# Optimizing a Trainium2 kernel written in Bass

```python
import numpy as np
import jax
import jax.numpy as jnp

def _softmax(x, axis=-1):
    return jax.nn.softmax(x, axis=axis)

def _gelu(x):
    return jax.nn.gelu(x, approximate=True)

def _silu(x):
    return jax.nn.silu(x)

def _sigmoid(x):
    return jax.nn.sigmoid(x)

def _layernorm(x, axis=-1, eps=1e-05):
    m = jnp.mean(x, axis=axis, keepdims=True)
    v = jnp.var(x, axis=axis, keepdims=True)
    return (x - m) / jnp.sqrt(v + eps)

def _scatter_add(tgt, idx, src, axis=0):
    return tgt.at[idx].add(src)

def _segment_sum(src, seg, n):
    return jax.ops.segment_sum(src, seg, n)
kernel_name = 'mk_sandwich_d1_jaxref_r8_5b6e8d'

def setup_inputs(seed: int=0):
    np.random.seed(seed)
    _w = jnp.asarray

    def _L0_attn_setup():
        import jax, jax.numpy as jnp
        import numpy as np
        D_MODEL, N_HEADS = (128, 16)
        D_H = D_MODEL // N_HEADS
        D_HR = D_H // 2
        D_LATENT = 32
        THETA = 10000.0

        def rope(x, theta=THETA):
            S, d = (x.shape[-2], x.shape[-1])
            inv = theta ** (-jnp.arange(0, d, 2, dtype=jnp.float32) / d)
            ang = jnp.arange(S, dtype=jnp.float32)[:, None] * inv
            cos, sin = (jnp.cos(ang), jnp.sin(ang))
            x1, x2 = (x[..., 0::2], x[..., 1::2])
            r1 = x1 * cos - x2 * sin
            r2 = x1 * sin + x2 * cos
            return jnp.stack([r1, r2], axis=-1).reshape(x.shape)
        key = jax.random.key(seed)
        ks = jax.random.split(key, 9)
        s = lambda fan_in: 1.0 / np.sqrt(fan_in)
        return {'x': jax.random.normal(ks[0], (4, 256, D_MODEL), jnp.float32), 'W_DQ': jax.random.normal(ks[1], (D_MODEL, D_LATENT), jnp.float32) * s(D_MODEL), 'W_UQ': jax.random.normal(ks[2], (D_LATENT, N_HEADS * D_H), jnp.float32) * s(D_LATENT), 'W_QR': jax.random.normal(ks[3], (D_LATENT, N_HEADS * D_HR), jnp.float32) * s(D_LATENT), 'W_DKV': jax.random.normal(ks[4], (D_MODEL, D_LATENT), jnp.float32) * s(D_MODEL), 'W_UK': jax.random.normal(ks[5], (D_LATENT, N_HEADS * D_H), jnp.float32) * s(D_LATENT), 'W_UV': jax.random.normal(ks[6], (D_LATENT, N_HEADS * D_H), jnp.float32) * s(D_LATENT), 'W_KR': jax.random.normal(ks[7], (D_MODEL, D_HR), jnp.float32) * s(D_MODEL), 'W_O': jax.random.normal(ks[8], (N_HEADS * D_H, D_MODEL), jnp.float32) * s(N_HEADS * D_H)}
    _L0_attn_in = _L0_attn_setup()

    def _L0_ffn_setup():
        import jax, jax.numpy as jnp
        import numpy as np
        D_IN, D_HID = (128, 512)

        def _ternary(key, shape):
            return jax.random.randint(key, shape, -1, 2).astype(jnp.float32)

        def _tlin(x, w, s):
            return jnp.einsum('bsi,oi->bso', x, w) * s
        key = jax.random.key(seed)
        ks = jax.random.split(key, 12)
        inv = lambda fan: 1.0 / np.sqrt(fan).astype(np.float32)
        return {'x': jax.random.normal(ks[0], (4, 256, D_IN), dtype=jnp.float32), 'w1_w': _ternary(ks[1], (D_HID, D_IN)), 'w1_s': jax.random.uniform(ks[2], (D_HID,), dtype=jnp.float32) * inv(D_IN), 'w2_w': _ternary(ks[3], (D_HID, D_IN)), 'w2_s': jax.random.uniform(ks[4], (D_HID,), dtype=jnp.float32) * inv(D_IN), 'h1_w': _ternary(ks[5], (D_HID, D_HID)), 'h1_s': jax.random.uniform(ks[6], (D_HID,), dtype=jnp.float32) * inv(D_HID), 'h2_w': _ternary(ks[7], (D_HID, D_HID)), 'h2_s': jax.random.uniform(ks[8], (D_HID,), dtype=jnp.float32) * inv(D_HID), 'w3_w': _ternary(ks[9], (D_IN, D_HID)), 'w3_s': jax.random.uniform(ks[10], (D_IN,), dtype=jnp.float32) * inv(D_HID)}
    _L0_ffn_in = _L0_ffn_setup()
    _d = {'L0_attn_x': _L0_attn_in['x'], 'L0_attn_W_DQ': _L0_attn_in['W_DQ'], 'L0_attn_W_UQ': _L0_attn_in['W_UQ'], 'L0_attn_W_QR': _L0_attn_in['W_QR'], 'L0_attn_W_DKV': _L0_attn_in['W_DKV'], 'L0_attn_W_UK': _L0_attn_in['W_UK'], 'L0_attn_W_UV': _L0_attn_in['W_UV'], 'L0_attn_W_KR': _L0_attn_in['W_KR'], 'L0_attn_W_O': _L0_attn_in['W_O'], 'L0_ffn_w1_w': _L0_ffn_in['w1_w'], 'L0_ffn_w1_s': _L0_ffn_in['w1_s'], 'L0_ffn_w2_w': _L0_ffn_in['w2_w'], 'L0_ffn_w2_s': _L0_ffn_in['w2_s'], 'L0_ffn_h1_w': _L0_ffn_in['h1_w'], 'L0_ffn_h1_s': _L0_ffn_in['h1_s'], 'L0_ffn_h2_w': _L0_ffn_in['h2_w'], 'L0_ffn_h2_s': _L0_ffn_in['h2_s'], 'L0_ffn_w3_w': _L0_ffn_in['w3_w'], 'L0_ffn_w3_s': _L0_ffn_in['w3_s']}
    _x0 = _d['L0_attn_x']
    _d['L0_attn_x'] = jax.random.normal(jax.random.fold_in(jax.random.key(seed), 1), (1, 2048, 128), dtype=_x0.dtype)
    del _x0
    return _d

def reference(L0_attn_x, L0_attn_W_DQ, L0_attn_W_UQ, L0_attn_W_QR, L0_attn_W_DKV, L0_attn_W_UK, L0_attn_W_UV, L0_attn_W_KR, L0_attn_W_O, L0_ffn_w1_w, L0_ffn_w1_s, L0_ffn_w2_w, L0_ffn_w2_s, L0_ffn_h1_w, L0_ffn_h1_s, L0_ffn_h2_w, L0_ffn_h2_s, L0_ffn_w3_w, L0_ffn_w3_s):

    def _L0_attn_ref(x, W_DQ, W_UQ, W_QR, W_DKV, W_UK, W_UV, W_KR, W_O):
        import jax, jax.numpy as jnp
        import numpy as np
        D_MODEL, N_HEADS = (128, 16)
        D_H = D_MODEL // N_HEADS
        D_HR = D_H // 2
        D_LATENT = 32
        THETA = 10000.0

        def rope(x, theta=THETA):
            S, d = (x.shape[-2], x.shape[-1])
            inv = theta ** (-jnp.arange(0, d, 2, dtype=jnp.float32) / d)
            ang = jnp.arange(S, dtype=jnp.float32)[:, None] * inv
            cos, sin = (jnp.cos(ang), jnp.sin(ang))
            x1, x2 = (x[..., 0::2], x[..., 1::2])
            r1 = x1 * cos - x2 * sin
            r2 = x1 * sin + x2 * cos
            return jnp.stack([r1, r2], axis=-1).reshape(x.shape)
        B, S, _ = x.shape
        d_qk = D_H + D_HR
        c_q = x @ W_DQ
        Qc = (c_q @ W_UQ).reshape(B, S, N_HEADS, D_H).transpose(0, 2, 1, 3)
        Qr = (c_q @ W_QR).reshape(B, S, N_HEADS, D_HR).transpose(0, 2, 1, 3)
        Qr = rope(Qr)
        c_kv = x @ W_DKV
        Kc = (c_kv @ W_UK).reshape(B, S, N_HEADS, D_H).transpose(0, 2, 1, 3)
        Kr = rope((x @ W_KR)[:, None, :, :])
        Kr = jnp.broadcast_to(Kr, (B, N_HEADS, S, D_HR))
        V = (c_kv @ W_UV).reshape(B, S, N_HEADS, D_H).transpose(0, 2, 1, 3)
        Q = jnp.concatenate([Qc, Qr], axis=-1)
        K = jnp.concatenate([Kc, Kr], axis=-1)
        scores = jnp.einsum('bhqd,bhkd->bhqk', Q, K)
        scores = jnp.clip(scores, -80.0, 80.0)
        causal = jnp.tril(jnp.ones((S, S), dtype=bool))
        scores = jnp.where(causal, scores, -jnp.inf)
        weights = jax.nn.softmax(scores / jnp.sqrt(jnp.float32(d_qk)), axis=-1)
        attn = jnp.einsum('bhqk,bhkd->bhqd', weights, V)
        attn = attn.transpose(0, 2, 1, 3).reshape(B, S, N_HEADS * D_H)
        return attn @ W_O

    def _L0_ffn_ref(x, w1_w, w1_s, w2_w, w2_s, h1_w, h1_s, h2_w, h2_s, w3_w, w3_s):
        import jax, jax.numpy as jnp
        import numpy as np
        D_IN, D_HID = (128, 512)

        def _ternary(key, shape):
            return jax.random.randint(key, shape, -1, 2).astype(jnp.float32)

        def _tlin(x, w, s):
            return jnp.einsum('bsi,oi->bso', x, w) * s
        h = jax.nn.silu(_tlin(x, w1_w, w1_s)) * _tlin(x, w2_w, w2_s)
        h = jax.nn.gelu(_tlin(h, h1_w, h1_s), approximate=False)
        h = jax.nn.gelu(_tlin(h, h2_w, h2_s), approximate=False)
        return _tlin(h, w3_w, w3_s)
    x = L0_attn_x
    x = x + _layernorm(_L0_attn_ref(_layernorm(x, axis=-1), L0_attn_W_DQ, L0_attn_W_UQ, L0_attn_W_QR, L0_attn_W_DKV, L0_attn_W_UK, L0_attn_W_UV, L0_attn_W_KR, L0_attn_W_O), axis=-1)
    x = x + _layernorm(_L0_ffn_ref(_layernorm(x, axis=-1), L0_ffn_w1_w, L0_ffn_w1_s, L0_ffn_w2_w, L0_ffn_w2_s, L0_ffn_h1_w, L0_ffn_h1_s, L0_ffn_h2_w, L0_ffn_h2_s, L0_ffn_w3_w, L0_ffn_w3_s), axis=-1)
    return x

_drawn_inputs = setup_inputs


def setup_inputs(seed=0):
    import zlib

    import numpy as np

    out = dict(_drawn_inputs(seed))
    spreads = {}
    factors = {}
    for name, (base, spread) in spreads.items():
        noise = np.random.default_rng([zlib.crc32(name.encode()), seed]).standard_normal(out[name].shape)
        drawn = base * np.exp(spread * noise) if base else spread * noise
        out[name] = jnp.asarray(drawn.astype(out[name].dtype))
    for name, factor in factors.items():
        out[name] = (out[name] * factor).astype(out[name].dtype)
    return out
```

```python
from contextlib import ExitStack

import numpy as np
import concourse.bass as bass
from concourse import mybir

F32 = mybir.dt.float32
F32R = mybir.dt.float32r
BF16 = mybir.dt.bfloat16
ALU = mybir.AluOpType
ACT = mybir.ActivationFunctionType

S = 2048
D = 128
H, DH, DR = 16, 8, 4
DQK = DH + DR
LAT = 32
HID = 512
MB = HID // 128
TILE = 512
NT = S // TILE
NB = TILE // 128
KB = S // 128
NQ = H // 4
PARTS = 3
ROWS = PARTS * PARTS * DQK
VW = DH + 1
EPS = 1e-5
SCALE = 1.0 / float(np.sqrt(np.float32(DQK)))
HI = float(np.exp(80.0 * SCALE))
LO = float(np.exp(-80.0 * SCALE))
PBUF = 4
SLOTS = 3


def steps():
    return [(t, kb, max(0, kb - NB * t) * 128) for t in range(NT) for kb in range(NB * (t + 1))]


STEPS = steps()
NSTEP = len(STEPS)
LAST = [NB * (t + 1) * (t + 2) // 2 for t in range(NT)]


def build(nc, x, wdown, wup, table, ident, mask, wo, w12, h12, w3, scales, out):
    with ExitStack() as ctx:
        def sb(name, shape, dt=F32, stack=ctx):
            return stack.enter_context(nc.sbuf_tensor(name, shape, dt))

        def sem(name):
            return ctx.enter_context(nc.semaphore(name))

        x_sb = sb("x_sb", [128, KB, D])
        attn = sb("attn", [128, KB, D])
        id_sb = sb("id_sb", [128, 128])
        wo_sb = sb("wo_sb", [128, D])
        sc_sb = sb("sc_sb", [128, 4 * MB + 1])
        w12h = sb("w12h", [128, 2, HID], F32R)
        w12l = sb("w12l", [128, 2, HID], F32R)
        h12h = sb("h12h", [128, 2, MB, HID], F32R)
        h12l = sb("h12l", [128, 2, MB, HID], F32R)
        w3h = sb("w3h", [128, MB, D], F32R)
        w3l = sb("w3l", [128, MB, D], F32R)
        stat = sb("stat", [128, NB, 6])
        mv = sb("mv", [128, NB, 2])
        var_eps = sb("var_eps", [128, NB])
        rstd = sb("rstd", [128, NB])
        neg_half = sb("neg_half", [128, NB])

        att = ExitStack()
        w_raw = sb("w_raw", [128, 2 * MB * HID], stack=att)
        v_all = sb("v_all", [128, KB, NQ, 4 * VW], stack=att)
        v_quad = sb("v_quad", [128, KB, 4, VW], stack=att)
        k_st = sb("k_st", [ROWS, 4, S], BF16, stack=att)
        q_st = sb("q_st", [ROWS, 4, S], BF16, stack=att)
        zeros = sb("zeros", [128, TILE], stack=att)
        msk = sb("msk", [128, 128], stack=att)
        acc_sb = sb("acc_sb", [128, TILE], stack=att)
        rcp = sb("rcp", [128, NB, 4], stack=att)
        proj = ExitStack()
        xn = sb("xn", [128, NB, D], stack=proj)
        xnT = sb("xnT", [128, TILE], stack=proj)
        wd_sb = sb("wd_sb", [128, 3 * 128], stack=proj)
        up_raw = sb("up_raw", [128, 512], stack=proj)
        up_sb = sb("up_sb", [128, 512], F32R, stack=proj)
        tab = sb("tab", [128, S], stack=proj)
        c_sb = [sb(f"c{i}_sb", [128, TILE], F32R, stack=proj) for i in range(2)]
        parts = [sb(f"part{i}", [128 if i < 2 else 64, PARTS, TILE], BF16, stack=proj) for i in range(4)]
        resid = [sb(f"resid{i}", [128 if i < 2 else 64, TILE], stack=proj) for i in range(4)]
        rope = [[sb(f"rope{i}{j}", [64, TILE], stack=proj) for j in range(3)] for i in range(2)]
        proj.close()
        p_sb = sb("p_sb", [128, PBUF, 4, TILE], stack=att)
        att.close()

        ffn = ExitStack()
        x1 = sb("x1", [128, KB, D], stack=ffn)
        xb = sb("xb", [128, NB, D], stack=ffn)
        nb = sb("nb", [128, NB], stack=ffn)
        attnT = sb("attnT", [128, TILE], stack=ffn)
        xn2 = sb("xn2", [128, NB, D], stack=ffn)
        xTh = sb("xTh", [128, S], F32R, stack=ffn)
        xTl = sb("xTl", [128, S], F32R, stack=ffn)
        g_h = [[sb(f"g{i}{j}h", [128, MB, TILE], F32R, stack=ffn) for j in range(2)] for i in range(2)]
        g_l = [[sb(f"g{i}{j}l", [128, MB, TILE], F32R, stack=ffn) for j in range(2)] for i in range(2)]
        g_f = [sb(f"gf{i}", [128, TILE], stack=ffn) for i in range(3)]
        s_f = [sb(f"sf{i}", [128, TILE], stack=ffn) for i in range(2)]
        u_f = sb("u_f", [128, TILE], stack=ffn)
        y_sb = sb("y_sb", [128, TILE], stack=ffn)
        o_sb = sb("o_sb", [128, NB, D], stack=ffn)
        ffn.close()

        ps = ctx.enter_context(nc.psum_tensor("ps", [128, 8, TILE], F32))
        B_TR, B_C, B_KR, B_QC, B_QR, B_KC, B_V = 0, 1, 3, 4, 5, 6, 7
        B_ACC = 6

        q_dram = nc.dram_tensor("q_parts", [H, PARTS, DQK, S], BF16).ap()
        k_dram = nc.dram_tensor("k_parts", [H, DQK, PARTS, S], BF16).ap()

        x_in = [sem(f"x_in{t}") for t in range(NT)]
        consts_in = sem("consts_in")
        ffnw_in = sem("ffnw_in")
        up_split = sem("up_split")
        ffnw_split = sem("ffnw_split")
        ones_set = sem("ones_set")
        ln_step = sem("ln_step")
        var_ready = sem("var_ready")
        stats_seen = sem("stats_seen")
        rstd_ready = sem("rstd_ready")
        xn_ready = sem("xn_ready")
        tr_done = sem("tr_done")
        xnT_ready = sem("xnT_ready")
        down_done = sem("down_done")
        c_hi = sem("c_hi")
        c_lo = sem("c_lo")
        up_done = sem("up_done")
        v_copied = sem("v_copied")
        rope_mul = sem("rope_mul")
        rope_done = sem("rope_done")
        part0 = sem("part0")
        resid0 = sem("resid0")
        part1 = sem("part1")
        part2 = sem("part2")
        parts_out = sem("parts_out")
        k_in = [sem(f"k_in{t}") for t in range(NT)]
        q_in = [sem(f"q_in{t}") for t in range(NT)]
        v_in = sem("v_in")
        scores_done = sem("scores_done")
        exp_done = sem("exp_done")
        clip_done = sem("clip_done")
        pv_done = sem("pv_done")
        acc_zero = sem("acc_zero")
        acc_out = sem("acc_out")
        accT_done = sem("accT_done")
        rcp_done = sem("rcp_done")
        attn_done = sem("attn_done")
        att_end = sem("att_end")
        at_done = sem("at_done")
        attnT_ready = sem("attnT_ready")
        wo_done = sem("wo_done")
        ln2_step = sem("ln2_step")
        xb_ready = sem("xb_ready")
        x1_ready = sem("x1_ready")
        xn2_ready = sem("xn2_ready")
        t2_done = sem("t2_done")
        xTh_ready = sem("xTh_ready")
        xTl_ready = sem("xTl_ready")
        ff_mm = sem("ff_mm")
        ff_act = sem("ff_act")
        ff_dve = sem("ff_dve")
        g_ready = sem("g_ready")
        hi_step = sem("hi_step")
        yT_done = sem("yT_done")
        ln3_step = sem("ln3_step")
        yb_ready = sem("yb_ready")
        o_ready = sem("o_ready")
        o_out = sem("o_out")

        block = ctx.enter_context(nc.Block())

        N_CONST = 7
        LN2, LN3 = 6, 3
        UPS = 4

        plan = [("up", a, m, g) for a in range(2) for m in range(MB) for g in range(2)]
        plan += [("h1", a, m, 0) for a in range(2) for m in range(MB)]
        plan += [("h2", a, m, 0) for a in range(2) for m in range(MB)]
        plan += [("down", a, 0, 0) for a in range(2)]
        FF_BANKS = 6
        n_act = n_dve = 0
        reader = []
        for stage, a, m, g in plan:
            if stage == "up" and g == 1:
                n_dve += 1
                reader.append(("dve", n_dve))
            else:
                n_act += 1
                reader.append(("act", n_act))
        N_MM, N_ACT, N_DVE = len(plan), n_act, n_dve
        N_G = 3 * 2 * MB

        def g_count(stage, a, m):
            return {"up": 0, "h1": 2 * MB, "h2": 4 * MB}[stage] + a * MB + m + 1

        @block.sync
        def _(sp):
            x_t = x.rearrange("o (t n p) d -> t p (o n) d", t=NT, p=128)
            sp.dma_start(x_sb[:, 0:NB, :], x_t[0]).then_inc(x_in[0], 16)
            sp.dma_start(id_sb[:], ident).then_inc(consts_in, 16)
            sp.dma_start(wd_sb[:], wdown).then_inc(consts_in, 16)
            sp.dma_start(up_raw[:], wup).then_inc(consts_in, 16)
            sp.dma_start(tab[:], table).then_inc(consts_in, 16)
            sp.dma_start(msk[:], mask).then_inc(consts_in, 16)
            sp.dma_start(wo_sb[:], wo).then_inc(consts_in, 16)
            sp.dma_start(sc_sb[:], scales).then_inc(consts_in, 16)
            for t in range(1, NT):
                sp.dma_start(x_sb[:, NB * t:NB * (t + 1), :], x_t[t]).then_inc(x_in[t], 16)
            sp.dma_start(w_raw[:, 0:2 * HID].rearrange("p (g m) -> p g m", g=2), w12.rearrange("g p m -> p g m")).then_inc(ffnw_in, 16)
            sp.dma_start(w_raw[:, 2 * HID:2 * HID + MB * D].rearrange("p (k m) -> p k m", k=MB),
                         w3.rearrange("(k p) m -> p k m", p=128)).then_inc(ffnw_in, 16)

            with sp.Fori(0, NT) as t:
                cols = bass.ds(t * TILE, TILE)
                for n in range(4):
                    sp.wait_ge(part2, t * 4 + n + 1)
                    is_k, d0, dn = n % 2, (0 if n < 2 else DH), (DH if n < 2 else DR)
                    for i in range(PARTS):
                        if is_k:
                            dst = k_dram[:, d0:d0 + dn, i, cols]
                        else:
                            dst = q_dram[:, i, d0:d0 + dn, cols]
                        sp.dma_start(dst, parts[n][:, i, :]).then_inc(parts_out, 16)

            def load_q(quad, t):
                for i in range(PARTS):
                    for j in range(4):
                        src = q_dram[bass.ds(quad * 4 + j, 1), i, :, t * TILE:(t + 1) * TILE]
                        src = src.rearrange("o d n -> (o d) n").unsqueeze(1).to_broadcast([DQK, PARTS, TILE])
                        sp.dma_start(q_st[i * PARTS * DQK:(i + 1) * PARTS * DQK, j, t * TILE:(t + 1) * TILE],
                                     src).then_inc(q_in[t], 16)

            def load_k(quad, t):
                for i in range(PARTS):
                    src = k_dram[bass.ds(quad * 4, 4), :, :, t * TILE:(t + 1) * TILE]
                    sp.dma_start(k_st[i * PARTS * DQK:(i + 1) * PARTS * DQK, :, t * TILE:(t + 1) * TILE],
                                 src.rearrange("h d j n -> (d j) h n")).then_inc(k_in[t], 16)

            sp.wait_ge(parts_out, 16 * NT * 4 * PARTS)
            for t in range(NT):
                load_k(0, t)
                load_q(0, t)
            sp.wait_ge(ffnw_split, 4)
            sp.dma_start(w_raw[:, :].rearrange("p (g k m) -> p g k m", g=2, k=MB), h12.rearrange("g (k p) m -> p g k m", p=128)).then_inc(ffnw_in, 16)
            with sp.Fori(0, NQ - 1) as q:
                for t in range(NT - 1):
                    sp.wait_ge(scores_done, q * (2 * NSTEP) + 2 * LAST[t])
                    load_q(q + 1, t)
                for c in range(NT):
                    sp.wait_ge(scores_done, q * (2 * NSTEP) + 2 * (LAST[NT - 2] + NB * (c + 1)))
                    load_k(q + 1, c)
                load_q(q + 1, NT - 1)

            with sp.Fori(0, NT) as t:
                sp.wait_ge(o_ready, t + 1)
                sp.dma_start(out.rearrange("o (n p) d -> p (o n) d", p=128)[:, bass.ds(t * NB, NB), :], o_sb[:]).then_inc(o_out, 16)
            sp.wait_ge(o_out, 16 * NT)

        @block.gpsimd
        def _(pool):
            pool.memset(v_all[:], 1.0).then_inc(ones_set, 1)
            pool.memset(neg_half[:], -0.5).then_inc(ones_set, 1)
            pool.memset(zeros[:], 0.0).then_inc(ones_set, 1)
            pool.wait_ge(ones_set, 3)

            def inverse_root(nth):
                pool.wait_ge(var_ready, nth + 1)
                pool.tensor_tensor(rstd[:], var_eps[:], neg_half[:], ALU.pow).then_inc(rstd_ready, 1)

            with pool.Fori(0, NT) as t:
                inverse_root(t)
                for n in range(4):
                    pool.wait_ge(resid0, t * 4 + n + 1)
                    pool.wait_ge(parts_out, t * (16 * 4 * PARTS))
                    pool.tensor_tensor(parts[n][:, 1, :], resid[n][:], zeros[0:resid[n].shape[0], :], ALU.add).then_inc(part1, 1)
                    pool.wait_ge(part1, t * 4 + n + 1)
                    pool.tensor_tensor(parts[n][:, 2, :], resid[n][:], parts[n][:, 1, :], ALU.subtract).then_inc(part2, 1)

            def v_stage(quad, c):
                return pool.tensor_tensor(v_quad[:, NB * c:NB * (c + 1), :, :].rearrange("p k h v -> p k (h v)"),
                                          v_all[:, NB * c:NB * (c + 1), bass.ds(quad, 1), :].rearrange("p k o v -> p k (o v)"),
                                          zeros[:, 0:NB * 4 * VW].rearrange("p (k v) -> p k v", k=NB), ALU.add)

            pool.wait_ge(v_copied, NT)
            for c in range(NT):
                v_stage(0, c).then_inc(v_in, 1)

            raw12 = w_raw[:, 0:2 * HID].rearrange("p (g m) -> p g m", g=2)
            raw3 = w_raw[:, 2 * HID:2 * HID + MB * D].rearrange("p (k m) -> p k m", k=MB)
            rawh = w_raw[:, :].rearrange("p (g k m) -> p g k m", g=2, k=MB)
            pool.wait_ge(ffnw_in, 32)
            pool.tensor_copy(w12h[:], raw12).then_inc(ffnw_split, 1)
            pool.tensor_copy(w3h[:], raw3).then_inc(ffnw_split, 1)
            pool.wait_ge(ffnw_split, 2)
            pool.tensor_tensor(w12l[:], raw12, w12h[:].bitcast(F32), ALU.subtract).then_inc(ffnw_split, 1)
            pool.tensor_tensor(w3l[:], raw3, w3h[:].bitcast(F32), ALU.subtract).then_inc(ffnw_split, 1)
            pool.wait_ge(ffnw_in, 48)
            pool.tensor_copy(h12h[:], rawh).then_inc(ffnw_split, 1)
            pool.wait_ge(ffnw_split, 5)
            pool.tensor_tensor(h12l[:], rawh, h12h[:].bitcast(F32), ALU.subtract).then_inc(ffnw_split, 1)

            with pool.Fori(0, NQ - 1) as q:
                for c in range(NT):
                    pool.wait_ge(pv_done, q * NSTEP + (LAST[NT - 2] + NB * (c + 1)))
                    v_stage(q + 1, c).then_inc(v_in, 1)

            with pool.Fori(NT, 4 * NT) as nth:
                inverse_root(nth)

        @block.scalar
        def _(act):
            with act.Fori(0, NT) as t:
                act.wait_ge(tr_done, t + 1)
                act.wait_ge(down_done, t * 3)
                act.activation(xnT[:], ps[:, B_TR, :], ACT.Copy).then_inc(xnT_ready, 1)
                for i in range(2):
                    act.wait_ge(down_done, t * 3 + i + 1)
                    act.wait_ge(up_done, t * UPS)
                    act.activation(c_sb[i][:], ps[:, B_C + i, :], ACT.Copy).then_inc(c_hi, 1)
                for n in range(2):
                    act.wait_ge(up_done, t * UPS + (1, 3)[n])
                    act.wait_ge(parts_out, t * (16 * 4 * PARTS))
                    act.activation(parts[n][:, 0, :], ps[:, (B_QC, B_KC)[n], :], ACT.Copy).then_inc(part0, 1)
                act.wait_ge(up_done, t * UPS + 4)
                act.wait_ge(ones_set, 3)
                for n in range(NB):
                    dst = v_all[:, bass.ds(t * NB + n, 1), :, :].rearrange("p o q (h v) -> p (o q h) v", v=VW)
                    cp = act.activation(dst[:, :, 0:DH], ps[:, B_V, n * 128:(n + 1) * 128].rearrange("p (h v) -> p h v", v=DH), ACT.Copy)
                cp.then_inc(v_copied, 1)
                for n in range(2, 4):
                    act.wait_ge(rope_done, t * 2 + n - 1)
                    act.activation(parts[n][:, 0, :], rope[n - 2][2][:], ACT.Copy).then_inc(part0, 1)

            act.wait_ge(part2, NT * 4)
            act.wait_ge(parts_out, 16 * NT * 4 * PARTS)
            with act.Fori(0, NQ) as q:
                for s, (t, kb, c0) in enumerate(STEPS):
                    act.wait_ge(pv_done, q * NSTEP + max(0, s - PBUF + 1))
                    for half in range(2):
                        h = 2 * s + half
                        act.wait_ge(scores_done, q * (2 * NSTEP) + h + 1)
                        slot = 2 * (h % SLOTS)
                        act.activation(p_sb[:, s % PBUF, 2 * half:2 * half + 2, c0:], ps[:, slot:slot + 2, c0:],
                                       ACT.Exp, scale=SCALE).then_inc(exp_done, 1)

            for t in range(NT):
                act.wait_ge(at_done, t + 1)
                act.wait_ge(wo_done, t)
                act.activation(attnT[:], ps[:, 0, :], ACT.Copy).then_inc(attnT_ready, 1)
                act.wait_ge(ln2_step, t * LN2 + 3)
                for n in range(NB):
                    i = act.activation(xb[:, n, :], x_sb[:, t * NB + n, :], ACT.Identity, bias=nb[:, n:n + 1])
                i.then_inc(xb_ready, 1)
                act.wait_ge(t2_done, t + 1)
                act.activation(xTh[:, t * TILE:(t + 1) * TILE], ps[:, 2, :], ACT.Copy).then_inc(xTh_ready, 1)

            with act.Fori(0, NT // 2) as u:
                n_s = n_g = 0
                for o, (stage, a, m, g) in enumerate(plan):
                    bank = o % FF_BANKS
                    if stage == "up":
                        if g == 1:
                            continue
                        act.wait_ge(ff_mm, u * N_MM + o + 1)
                        act.wait_ge(ff_dve, u * N_DVE + max(0, n_s - 1))
                        act.activation(s_f[n_s % 2][:], ps[:, bank, :], ACT.Silu, scale=sc_sb[:, m:m + 1]).then_inc(ff_act, 1)
                        n_s += 1
                    elif stage == "down":
                        act.wait_ge(ff_mm, u * N_MM + o + 1)
                        act.wait_ge(yT_done, u * 2 + a)
                        act.activation(y_sb[:], ps[:, bank, :], ACT.Copy, scale=sc_sb[:, 4 * MB:4 * MB + 1]).then_inc(ff_act, 1)
                        act.wait_ge(ln3_step, (u * 2 + a) * LN3 + 3)
                        for n in range(NB):
                            i = act.activation(xb[:, n, :], x1[:, bass.ds((u * 2 + a) * NB + n, 1), :].rearrange("p o d -> p (o d)"), ACT.Identity, bias=nb[:, n:n + 1])
                        i.then_inc(yb_ready, 1)
                    else:
                        k = {"h1": 2, "h2": 3}[stage]
                        act.wait_ge(ff_mm, u * N_MM + o + 1)
                        act.wait_ge(g_ready, u * N_G + max(0, 2 * MB + n_g - 2))
                        act.activation(g_f[n_g % 3][:], ps[:, bank, :], ACT.Gelu, scale=sc_sb[:, k * MB + m:k * MB + m + 1]).then_inc(ff_act, 1)
                        n_g += 1

        @block.vector
        def _(dve):
            dve.wait_ge(consts_in, 16 * N_CONST)
            dve.tensor_copy(up_sb[:], up_raw[:]).then_inc(up_split, 1)
            dve.wait_ge(up_split, 1)
            for g in (1, 3):
                r = slice(32 * g, 32 * g + 32)
                dve.tensor_tensor(up_sb[r, :], up_raw[r, :], up_sb[r, :].bitcast(F32), ALU.subtract).then_inc(up_split, 1)
            for t in range(1, NT):
                dve.wait_ge(x_in[t], 16)
            dve.wait_ge(x_in[0], 16)

            def layer_norm_stats(src, steps_sem, base, nth):
                for n in range(NB):
                    i = dve.bn_stats(stat[:, n, :], src(n))
                i.then_inc(steps_sem, 1)
                dve.wait_ge(steps_sem, base + 1)
                dve.sem_inc(stats_seen, 1)
                for n in range(NB):
                    i = dve.bn_aggr(mv[:, n, :], stat[:, n, :])
                i.then_inc(steps_sem, 1)
                dve.wait_ge(steps_sem, base + 2)
                dve.tensor_scalar(var_eps[:], mv[:, :, 1], EPS, None, ALU.add).then_inc(var_ready, 1)
                dve.wait_ge(rstd_ready, nth + 1)

            with dve.Fori(0, NT) as t:
                layer_norm_stats(lambda n: x_sb[:, bass.ds(t * NB + n, 1), :].rearrange("p o d -> p (o d)"), ln_step, t * 2, t)
                dve.wait_ge(tr_done, t)
                for n in range(NB):
                    i = dve.tensor_scalar(xn[:, n, :], x_sb[:, bass.ds(t * NB + n, 1), :].rearrange("p o d -> p (o d)"),
                                          mv[:, n, 0:1], rstd[:, n:n + 1], ALU.subtract, ALU.mult)
                i.then_inc(xn_ready, 1)
                for i in range(2):
                    dve.wait_ge(c_hi, t * 2 + i + 1)
                    dve.tensor_tensor(c_sb[i][64:128, :], ps[64:128, B_C + i, :], c_sb[i][64:128, :].bitcast(F32),
                                      ALU.subtract).then_inc(c_lo, 1)
                for i, (bank, ready) in enumerate(((B_QR, (up_done, t * UPS + 2)), (B_KR, (down_done, t * 3 + 3)))):
                    dve.wait_ge(*ready)
                    dve.wait_ge(part0, t * 4)
                    dve.tensor_tensor(rope[i][0][:], ps[0:64, bank, :], tab[0:64, bass.ds(t * TILE, TILE)], ALU.mult)
                    dve.tensor_tensor(rope[i][1][:], ps[64:128, bank, :], tab[64:128, bass.ds(t * TILE, TILE)], ALU.mult).then_inc(rope_mul, 1)
                    dve.wait_ge(rope_mul, t * 2 + i + 1)
                    dve.tensor_tensor(rope[i][2][:], rope[i][0][:], rope[i][1][:], ALU.add).then_inc(rope_done, 1)
                for n in range(4):
                    dve.wait_ge(part0, t * 4 + n + 1)
                    dve.wait_ge(part2, t * 4)
                    src = ps[:, (B_QC, B_KC)[n], :] if n < 2 else rope[n - 2][2][:]
                    dve.tensor_tensor(resid[n][:], src, parts[n][:, 0, :], ALU.subtract).then_inc(resid0, 1)

            dve.wait_ge(v_copied, NT)
            dve.wait_ge(resid0, 4 * NT)
            dve.memset(ps[:, B_ACC:B_ACC + 2, :], 0.0).then_inc(acc_zero, 1)
            dve.wait_ge(acc_zero, 1)

            def clip(q, s, half):
                t, kb, c0 = STEPS[s]
                dve.wait_ge(exp_done, q * (2 * NSTEP) + 2 * s + half + 1)
                p = p_sb[:, s % PBUF, 2 * half:2 * half + 2, :]
                if kb < NB * t:
                    i = dve.tensor_scalar(p, p, LO, HI, ALU.max, ALU.min)
                else:
                    d = p[:, :, c0:c0 + 128]
                    i = dve.scalar_tensor_tensor(d, d, LO, msk[:].unsqueeze(1).to_broadcast([128, 2, 128]), ALU.max, ALU.min)
                    if c0 + 128 < TILE:
                        r = p[:, :, c0 + 128:]
                        i = dve.tensor_scalar(r, r, LO, HI, ALU.max, ALU.min)
                i.then_inc(clip_done, 1)

            def evacuate(q, t):
                dve.wait_ge(pv_done, q * NSTEP + LAST[t])
                dve.wait_ge(accT_done, q * NT + t)
                dve.tensor_copy(acc_sb[:], ps[:, B_ACC + t % 2, :]).then_inc(acc_out, 1)

            def normalise(q, t):
                dve.wait_ge(accT_done, q * NT + t + 1)
                bank = ps[:, B_ACC + t % 2, :].rearrange("p (n h v) -> p n h v", n=NB, h=4)
                dve.reciprocal(rcp[:], bank[:, :, :, DH]).then_inc(rcp_done, 1)
                dve.wait_ge(rcp_done, q * NT + t + 1)
                dst = attn[:, NB * t:NB * (t + 1), bass.ds(q * (4 * DH), 4 * DH)].rearrange("p n (h v) -> p n h v", h=4)
                dve.tensor_tensor(dst, bank[:, :, :, 0:DH], rcp[:].unsqueeze(3).to_broadcast([128, NB, 4, DH]), ALU.mult).then_inc(attn_done, 1)

            with dve.Fori(0, NQ) as q:
                for s, (t, kb, c0) in enumerate(STEPS):
                    for half in range(2):
                        clip(q, s, half)
                    if t > 0 and kb == 2:
                        evacuate(q, t - 1)
                    if t > 0 and kb == 5:
                        normalise(q, t - 1)
                evacuate(q, NT - 1)
                normalise(q, NT - 1)

            for t in range(NT):
                dve.wait_ge(wo_done, t + 1)
                layer_norm_stats(lambda n: ps[:, 1, n * D:(n + 1) * D], ln2_step, t * LN2, NT + 2 * t)
                dve.scalar_tensor_tensor(nb[:], mv[:, :, 0], -1.0, rstd[:], ALU.mult, ALU.mult).then_inc(ln2_step, 1)
                dve.wait_ge(xb_ready, t + 1)
                for n in range(NB):
                    i = dve.scalar_tensor_tensor(x1[:, t * NB + n, :], ps[:, 1, n * D:(n + 1) * D], rstd[:, n:n + 1], xb[:, n, :], ALU.mult, ALU.add)
                i.then_inc(ln2_step, 1)
                dve.wait_ge(ln2_step, t * LN2 + 4)
                layer_norm_stats(lambda n: x1[:, t * NB + n, :], ln2_step, t * LN2 + 4, NT + 2 * t + 1)
                dve.wait_ge(t2_done, t)
                for n in range(NB):
                    i = dve.tensor_scalar(xn2[:, n, :], x1[:, t * NB + n, :], mv[:, n, 0:1], rstd[:, n:n + 1], ALU.subtract, ALU.mult)
                i.then_inc(xn2_ready, 1)
                dve.wait_ge(xTh_ready, t + 1)
                dve.tensor_tensor(xTl[:, t * TILE:(t + 1) * TILE], ps[:, 2, :], xTh[:, t * TILE:(t + 1) * TILE].bitcast(F32),
                                  ALU.subtract).then_inc(xTl_ready, 1)

            def split_g(full, hi, lo, hi_count):
                dve.tensor_copy(hi, full).then_inc(hi_step, 1)
                dve.wait_ge(hi_step, hi_count)
                dve.tensor_tensor(lo, full, hi.bitcast(F32), ALU.subtract).then_inc(g_ready, 1)

            with dve.Fori(0, NT // 2) as u:
                n_g = n_hi = 0
                for o, (stage, a, m, g) in enumerate(plan):
                    bank = o % FF_BANKS
                    engine, count = reader[o]
                    if stage == "up" and g == 1:
                        dve.wait_ge(ff_mm, u * N_MM + o + 1)
                        dve.wait_ge(ff_act, u * N_ACT + reader[o - 1][1])
                        dve.wait_ge(g_ready, u * N_G + n_hi)
                        dve.scalar_tensor_tensor(u_f[:], ps[:, bank, :], sc_sb[:, MB + m:MB + m + 1], s_f[(count - 1) % 2][:],
                                                 ALU.mult, ALU.mult).then_inc(ff_dve, 1)
                        dve.wait_ge(ff_dve, u * N_DVE + count)
                        n_hi += 1
                        split_g(u_f[:], g_h[0][a][:, m, :], g_l[0][a][:, m, :], u * N_G + n_hi)
                    elif stage in ("h1", "h2"):
                        gen = {"h1": 1, "h2": 0}[stage]
                        dve.wait_ge(ff_act, u * N_ACT + count)
                        n_hi += 1
                        split_g(g_f[n_g % 3][:], g_h[gen][a][:, m, :], g_l[gen][a][:, m, :], u * N_G + n_hi)
                        n_g += 1
                    elif stage == "down":
                        tile = u * 2 + a
                        dve.wait_ge(yT_done, tile + 1)
                        layer_norm_stats(lambda n: ps[:, 6 + a, n * D:(n + 1) * D], ln3_step, tile * LN3, 3 * NT + tile)
                        dve.scalar_tensor_tensor(nb[:], mv[:, :, 0], -1.0, rstd[:], ALU.mult, ALU.mult).then_inc(ln3_step, 1)
                        dve.wait_ge(yb_ready, tile + 1)
                        dve.wait_ge(o_out, tile * 16)
                        for n in range(NB):
                            i = dve.scalar_tensor_tensor(o_sb[:, n, :], ps[:, 6 + a, n * D:(n + 1) * D], rstd[:, n:n + 1], xb[:, n, :], ALU.mult, ALU.add)
                        i.then_inc(o_ready, 1)

        @block.tensor
        def _(pe):
            pe.wait_ge(consts_in, 16 * N_CONST)
            pe.wait_ge(up_split, 3)

            with pe.Fori(0, NT) as t:
                pe.wait_ge(xn_ready, t + 1)
                pe.wait_ge(xnT_ready, t)
                for n in range(NB):
                    i = pe.transpose(ps[:, B_TR, n * 128:(n + 1) * 128], xn[:, n, :], id_sb[:])
                i.then_inc(tr_done, 1)
                pe.wait_ge(xnT_ready, t + 1)
                pe.wait_ge(c_lo, t * 2)
                for i in range(2):
                    pe.matmul(ps[:, B_C + i, :], wd_sb[:, i * 128:(i + 1) * 128], xnT[:], start=True, stop=True).then_inc(down_done, 1)
                pe.wait_ge(rope_mul, t * 2)
                pe.matmul(ps[:, B_KR, :], wd_sb[:, 256:384], xnT[:], start=True, stop=True).then_inc(down_done, 1)
                pe.wait_ge(c_lo, t * 2 + 1)
                pe.wait_ge(resid0, t * 4)
                pe.matmul(ps[:, B_QC, :], up_sb[:, 0:128], c_sb[0][:], start=True, stop=True).then_inc(up_done, 1)
                pe.matmul(ps[:, B_QR, :], up_sb[:, 128:256], c_sb[0][:], start=True, stop=True).then_inc(up_done, 1)
                pe.wait_ge(c_lo, t * 2 + 2)
                pe.matmul(ps[:, B_KC, :], up_sb[:, 256:384], c_sb[1][:], start=True, stop=True).then_inc(up_done, 1)
                pe.wait_ge(v_copied, t)
                for n in range(NB):
                    i = pe.matmul(ps[:, B_V, n * 128:(n + 1) * 128], c_sb[1][:, n * 128:(n + 1) * 128], up_sb[:, 384:512], start=True, stop=True)
                i.then_inc(up_done, 1)

            def scores(q, h):
                s, half = h // 2, h % 2
                t, kb, c0 = STEPS[s]
                if kb == 0 and half == 0:
                    pe.wait_ge(q_in[t], (q + 1) * (16 * PARTS * 4))
                if kb == NB * t and half == 0:
                    pe.wait_ge(k_in[t], (q + 1) * (16 * PARTS))
                pe.wait_ge(exp_done, q * (2 * NSTEP) + max(0, h - SLOTS + 1))
                for j in range(2):
                    i = pe.matmul(ps[:, 2 * (h % SLOTS) + j, c0:], k_st[:, 2 * half + j, kb * 128:(kb + 1) * 128],
                                  q_st[:, 2 * half + j, t * TILE + c0:(t + 1) * TILE], start=True, stop=True)
                i.then_inc(scores_done, 1)

            def weigh(q, s):
                t, kb, c0 = STEPS[s]
                pe.wait_ge(clip_done, q * (2 * NSTEP) + 2 * s + 2)
                if kb == NB * t:
                    pe.wait_ge(v_in, q * NT + t + 1)
                if kb == 0:
                    pe.wait_ge(attn_done, q * NT + max(0, t - 1))
                for j in range(4):
                    i = pe.matmul(ps[32 * j:32 * j + VW, B_ACC + t % 2, c0:], v_quad[:, kb, j, :], p_sb[:, s % PBUF, j, c0:],
                                  start=(kb == 0), stop=(kb == NB * (t + 1) - 1))
                i.then_inc(pv_done, 1)

            def turn(q, t):
                pe.wait_ge(acc_out, q * NT + t + 1)
                for n in range(NB):
                    i = pe.transpose(ps[:, B_ACC + t % 2, n * 128:(n + 1) * 128], acc_sb[:, n * 128:(n + 1) * 128], id_sb[:])
                i.then_inc(accT_done, 1)

            LAG = 2
            pe.wait_ge(resid0, 4 * NT)
            pe.wait_ge(v_copied, NT)
            pe.wait_ge(acc_zero, 1)
            with pe.Fori(0, NQ) as q:
                for s in range(NSTEP + LAG):
                    if s < NSTEP:
                        scores(q, 2 * s)
                        scores(q, 2 * s + 1)
                    if s >= LAG:
                        weigh(q, s - LAG)
                        t, kb, _ = STEPS[s - LAG]
                        if t > 0 and kb == 2:
                            turn(q, t - 1)
                turn(q, NT - 1)

            pe.wait_ge(attn_done, NQ * NT)
            for t in range(NT):
                for n in range(NB):
                    i = pe.transpose(ps[:, 0, n * 128:(n + 1) * 128], attn[:, t * NB + n, :], id_sb[:])
                i.then_inc(at_done, 1)
                pe.wait_ge(attnT_ready, t + 1)
                pe.wait_ge(ln2_step, max(0, (t - 1) * LN2 + 4))
                for n in range(NB):
                    i = pe.matmul(ps[:, 1, n * D:(n + 1) * D], attnT[:, n * 128:(n + 1) * 128], wo_sb[:], start=True, stop=True)
                i.then_inc(wo_done, 1)
                pe.wait_ge(xn2_ready, t + 1)
                pe.wait_ge(xTl_ready, t)
                for n in range(NB):
                    i = pe.transpose(ps[:, 2, n * 128:(n + 1) * 128], xn2[:, n, :], id_sb[:])
                i.then_inc(t2_done, 1)

            pe.wait_ge(ffnw_split, 6)
            pe.wait_ge(xTl_ready, NT)

            def product(bank, terms):
                n, last = 0, 3 * len(terms) - 1
                for wait, wh, wl, ah, al in terms:
                    if wait is not None:
                        pe.wait_ge(g_ready, wait)
                    for w, v in ((wh, ah), (wh, al), (wl, ah)):
                        i = pe.matmul(ps[:, bank, :], w, v, start=(n == 0), stop=(n == last))
                        n += 1
                i.then_inc(ff_mm, 1)

            with pe.Fori(0, NT // 2) as u:
                for o, (stage, a, m, g) in enumerate(plan):
                    bank = o % FF_BANKS
                    if o < FF_BANKS:
                        pe.wait_ge(ff_act, u * N_ACT)
                        pe.wait_ge(ff_dve, u * N_DVE)
                    else:
                        engine, count = reader[o - FF_BANKS]
                        if engine == "act":
                            pe.wait_ge(ff_act, u * N_ACT + count)
                        else:
                            pe.wait_ge(ff_dve, u * N_DVE + count)
                    cols = slice(m * 128, (m + 1) * 128)
                    if stage == "up":
                        tok = bass.ds((u * 2 + a) * TILE, TILE)
                        product(bank, [(None, w12h[:, g, cols], w12l[:, g, cols], xTh[:, tok], xTl[:, tok])])
                    elif stage == "h1":
                        product(bank, [(u * N_G + g_count("up", a, k), h12h[:, 0, k, cols], h12l[:, 0, k, cols],
                                        g_h[0][a][:, k, :], g_l[0][a][:, k, :]) for k in range(MB)])
                    elif stage == "h2":
                        product(bank, [(u * N_G + g_count("h1", a, k), h12h[:, 1, k, cols], h12l[:, 1, k, cols],
                                        g_h[1][a][:, k, :], g_l[1][a][:, k, :]) for k in range(MB)])
                    else:
                        product(bank, [(u * N_G + g_count("h2", a, k), w3h[:, k, :], w3l[:, k, :],
                                        g_h[0][a][:, k, :], g_l[0][a][:, k, :]) for k in range(MB)])
                for a in range(2):
                    pe.wait_ge(ff_act, u * N_ACT + reader[N_MM - 2 + a][1])
                    pe.wait_ge(o_ready, u * 2)
                    for n in range(NB):
                        i = pe.transpose(ps[:, 6 + a, n * 128:(n + 1) * 128], y_sb[:, n * 128:(n + 1) * 128], id_sb[:])
                    i.then_inc(yT_done, 1)


def kernel(L0_attn_x, L0_attn_W_DQ, L0_attn_W_UQ, L0_attn_W_QR, L0_attn_W_DKV, L0_attn_W_UK, L0_attn_W_UV,
           L0_attn_W_KR, L0_attn_W_O, L0_ffn_w1_w, L0_ffn_w1_s, L0_ffn_w2_w, L0_ffn_w2_s, L0_ffn_h1_w, L0_ffn_h1_s,
           L0_ffn_h2_w, L0_ffn_h2_s, L0_ffn_w3_w, L0_ffn_w3_s):
    import concourse.bacc as bacc
    from concourse.bass_utils import run_bass_kernel_spmd

    a = np.asarray
    swap = np.arange(H * DR) ^ 1
    kr = np.tile(a(L0_attn_W_KR), (1, H))
    wup = np.concatenate([a(L0_attn_W_UQ), a(L0_attn_W_QR), a(L0_attn_W_QR)[:, swap], a(L0_attn_W_UK), a(L0_attn_W_UV)], axis=1)
    inv = np.float32(10000.0) ** (-np.arange(0, DR, 2, dtype=np.float32) / np.float32(DR))
    angle = (np.arange(S, dtype=np.float32)[:, None] * inv).T.astype(np.float64)
    cos = np.repeat(np.cos(angle), 2, axis=0)
    sin = np.repeat(np.sin(angle), 2, axis=0) * np.array([-1.0, 1.0, -1.0, 1.0])[:, None]
    arrays = {
        "x": a(L0_attn_x),
        "wdown": np.concatenate([np.tile(a(L0_attn_W_DQ), (1, 4)), np.tile(a(L0_attn_W_DKV), (1, 4)), kr, kr[:, swap]], axis=1),
        "wup": np.tile(wup, (4, 1)),
        "table": np.concatenate([np.tile(cos, (H, 1)), np.tile(sin, (H, 1))]).astype(np.float32),
        "ident": np.eye(128, dtype=np.float32),
        "mask": np.where(np.arange(128)[None, :] >= np.arange(128)[:, None], np.float32(HI), np.float32(0)),
        "wo": a(L0_attn_W_O),
        "w12": np.stack([a(L0_ffn_w1_w).T, a(L0_ffn_w2_w).T]),
        "h12": np.stack([a(L0_ffn_h1_w).T, a(L0_ffn_h2_w).T]),
        "w3": a(L0_ffn_w3_w).T,
"scales": np.concatenate([a(v).reshape(-1, 128) for v in (L0_ffn_w1_s, L0_ffn_w2_s, L0_ffn_h1_s, L0_ffn_h2_s, L0_ffn_w3_s)]).T,
    }
    nc = bacc.Bacc("TRN2", target_bir_lowering=False, num_devices=1)
    ins, args = {}, {}
    for name, v in arrays.items():
        v = np.ascontiguousarray(v)
        ins["in_" + name] = v
        args[name] = nc.dram_tensor("in_" + name, v.shape, F32, kind="ExternalInput").ap()
    args["out"] = nc.dram_tensor("out", (1, S, D), F32, kind="ExternalOutput").ap()
    build(nc, **args)
    r = run_bass_kernel_spmd(nc, [ins], core_ids=[0])
    return r.results[0]["out"]
```

```python
from contextlib import ExitStack

import numpy as np
import concourse.bass as bass
from concourse import mybir

F32 = mybir.dt.float32
F32R = mybir.dt.float32r
BF16 = mybir.dt.bfloat16
ALU = mybir.AluOpType
ACT = mybir.ActivationFunctionType

S = 2048
D = 128
H, DH, DR = 16, 8, 4
DQK = DH + DR
LAT = 32
HID = 512
MB = HID // 128
TILE = 512
NT = S // TILE
NB = TILE // 128
KB = S // 128
NQ = H // 4
PARTS = 3
ROWS = PARTS * PARTS * DQK
VW = DH + 1
EPS = 1e-5
SCALE = 1.0 / float(np.sqrt(np.float32(DQK)))
HI = float(np.exp(80.0 * SCALE))
LO = float(np.exp(-80.0 * SCALE))
PBUF = 4
SLOTS = 3


def steps():
    return [(t, kb, max(0, kb - NB * t) * 128) for t in range(NT) for kb in range(NB * (t + 1))]


STEPS = steps()
NSTEP = len(STEPS)
LAST = [NB * (t + 1) * (t + 2) // 2 for t in range(NT)]
EDGE = 7
LAG = 2
SLOT = [h % SLOTS for h in range(2 * NSTEP)]
SLOT_USED = [max(u for u in range(h - 2 * NSTEP, h) if SLOT[u % (2 * NSTEP)] == SLOT[h]) + 1 for h in range(2 * NSTEP)]
LNB = 4
LN2_ORDER = [("att", 0), ("att", 1), ("ffn", 0), ("ffn", 1), ("att", 2), ("att", 3), ("ffn", 2), ("ffn", 3)]
LN2_NTH = {what: NT + n for n, what in enumerate(LN2_ORDER)}
LN2_SLOT = {what: (NT + n) % LNB for n, what in enumerate(LN2_ORDER)}


def build(nc, x, wdown, wup, table, ident, mask, wo, w12, h12, w3, scales, out):
    with ExitStack() as ctx:
        def sb(name, shape, dt=F32, stack=ctx):
            return stack.enter_context(nc.sbuf_tensor(name, shape, dt))

        def sem(name):
            return ctx.enter_context(nc.semaphore(name))

        x_sb = sb("x_sb", [128, KB, D])
        attn = sb("attn", [128, KB, D])
        id_sb = sb("id_sb", [128, 128])
        wo_sb = sb("wo_sb", [128, D])
        sc_sb = sb("sc_sb", [128, 4 * MB + 1])
        w12h = sb("w12h", [128, 2, HID], F32R)
        w12l = sb("w12l", [128, 2, HID], F32R)
        h12h = sb("h12h", [128, 2, MB, HID], F32R)
        h12l = sb("h12l", [128, 2, MB, HID], F32R)
        w3h = sb("w3h", [128, MB, D], F32R)
        w3l = sb("w3l", [128, MB, D], F32R)
        stat = sb("stat", [128, LNB, NB, 6])
        mv = sb("mv", [128, LNB, NB, 2])
        var_eps = sb("var_eps", [128, LNB, NB])
        rstd = sb("rstd", [128, LNB, NB])
        nb = sb("nb", [128, LNB, NB])
        neg_half = sb("neg_half", [128, NB])
        lo_max = sb("lo_max", [128, 6])
        lo_any = sb("lo_any", [128, 1])
        ones_col = sb("ones_col", [128, 1])
        lo_flag = sb("lo_flag", [1, 1])

        att = ExitStack()
        w_raw = sb("w_raw", [128, 2 * MB * HID], stack=att)
        v_all = sb("v_all", [128, KB, NQ, 4 * VW], stack=att)
        v_quad = sb("v_quad", [128, KB, 4, VW], stack=att)
        k_st = sb("k_st", [ROWS, 4, S], BF16, stack=att)
        q_st = sb("q_st", [ROWS, 4, S], BF16, stack=att)
        msk = sb("msk", [128, 128], stack=att)
        acc_sb = sb("acc_sb", [128, TILE], stack=att)
        rcp = sb("rcp", [128, NB, 4], stack=att)
        zeros = sb("zeros", [128, NB * 4 * VW], stack=att)
        wd_sb = sb("wd_sb", [128, 3 * 128], stack=att)
        up_raw = sb("up_raw", [128, 512], stack=att)
        up_sb = sb("up_sb", [128, 512], F32R, stack=att)
        parts = [[sb(f"part{n}{b}", [128, PARTS, TILE], BF16, stack=att) for b in range(2)] for n in range(3)]
        resid = [[sb(f"resid{n}{b}", [128, TILE], stack=att) for b in range(2)] for n in range(3)]
        rope = [sb(f"rope{i}", [128, TILE], stack=att) for i in range(3)]
        proj = ExitStack()
        xn = sb("xn", [128, KB, D], stack=proj)
        xnT = sb("xnT", [128, 2, TILE], stack=proj)
        tab = sb("tab", [128, NT, 2, TILE], stack=proj)
        c_sb = [sb(f"c{i}_sb", [128, TILE], F32R, stack=proj) for i in range(2)]
        proj.close()
        p_sb = sb("p_sb", [128, PBUF, 4, TILE], stack=att)
        att.close()

        ffn = ExitStack()
        x1 = sb("x1", [128, KB, D], stack=ffn)
        yb = sb("yb", [128, 2, NB, D], stack=ffn)
        attnT = sb("attnT", [128, 2, TILE], stack=ffn)
        xn2 = sb("xn2", [128, 2, NB, D], stack=ffn)
        xTh = sb("xTh", [128, S], F32R, stack=ffn)
        xTl = sb("xTl", [128, S], F32R, stack=ffn)
        g_h = [[sb(f"g{i}{j}h", [128, MB, TILE], F32R, stack=ffn) for j in range(2)] for i in range(2)]
        g_l = [[sb(f"g{i}{j}l", [128, MB, TILE], F32R, stack=ffn) for j in range(2)] for i in range(2)]
        g_f = [sb(f"gf{i}", [128, TILE], stack=ffn) for i in range(3)]
        s_f = [sb(f"sf{i}", [128, TILE], stack=ffn) for i in range(2)]
        u_f = [sb(f"uf{i}", [128, TILE], stack=ffn) for i in range(2)]
        y_sb = [sb(f"y_sb{i}", [128, TILE], stack=ffn) for i in range(2)]
        ffn.close()

        ps = ctx.enter_context(nc.psum_tensor("ps", [128, 8, TILE], F32))
        B_TR, B_C, B_RA, B_RB, B_QC, B_KC, B_V = 0, 1, 3, 4, 5, 6, 7
        B_ACC = 6
        B_AT, B_WO, B_T2 = 0, 2, 6
        FF_BANKS, B_YT = 6, 6

        q_dram = nc.dram_tensor("q_parts", [H, PARTS, DQK, S], BF16).ap()
        k_dram = nc.dram_tensor("k_parts", [H * DH, PARTS, S], BF16).ap()
        kr_dram = nc.dram_tensor("kr_parts", [DR, PARTS, S], BF16).ap()

        x_in = [sem(f"x_in{t}") for t in range(NT)]
        tab_in = [sem(f"tab_in{t}") for t in range(NT)]
        id_in = sem("id_in")
        wd_in = sem("wd_in")
        up_in = sem("up_in")
        late_in = sem("late_in")
        ffnw_in = [sem(f"ffnw_in{i}") for i in range(2)]
        up_split = sem("up_split")
        ffnw_split = sem("ffnw_split")
        filled = sem("filled")
        stats_done = sem("stats_done")
        stats_seen = sem("stats_seen")
        mv_done = sem("mv_done")
        var_ready = sem("var_ready")
        rstd_ready = sem("rstd_ready")
        nb_ready = sem("nb_ready")
        xn_ready = sem("xn_ready")
        tr_done = sem("tr_done")
        xnT_ready = sem("xnT_ready")
        down_done = sem("down_done")
        c_hi = sem("c_hi")
        c_lo = sem("c_lo")
        up_done = sem("up_done")
        v_copied = sem("v_copied")
        rope_mul = sem("rope_mul")
        rope_done = sem("rope_done")
        part0 = [sem(f"part0_{n}") for n in range(3)]
        resid0 = [sem(f"resid0_{n}") for n in range(3)]
        part1 = [sem(f"part1_{n}") for n in range(3)]
        part2 = [sem(f"part2_{n}") for n in range(3)]
        parts_out = [sem(f"parts_out{t}") for t in range(NT)]
        k_in = [sem(f"k_in{t}") for t in range(NT)]
        q_in = [sem(f"q_in{t}") for t in range(NT)]
        v_in = sem("v_in")
        scores_done = sem("scores_done")
        exp_done = sem("exp_done")
        clip_done = sem("clip_done")
        pv_done = sem("pv_done")
        acc_zero = sem("acc_zero")
        acc_out = sem("acc_out")
        accT_done = sem("accT_done")
        rcp_done = sem("rcp_done")
        attn_done = sem("attn_done")
        lo_step = sem("lo_step")
        flag_mm = sem("flag_mm")
        flag_ready = sem("flag_ready")
        at_done = sem("at_done")
        attnT_ready = sem("attnT_ready")
        wo_done = sem("wo_done")
        yb_ready = sem("yb_ready")
        x1_ready = sem("x1_ready")
        xn2_ready = sem("xn2_ready")
        t2_done = sem("t2_done")
        xTh_ready = sem("xTh_ready")
        xTl_ready = sem("xTl_ready")
        ff_mm = sem("ff_mm")
        ff_act = sem("ff_act")
        ff_dve = sem("ff_dve")
        gh_ready = sem("gh_ready")
        g_ready = sem("g_ready")
        uh_ready = sem("uh_ready")
        yT_done = sem("yT_done")
        o_ready = sem("o_ready")
        o_out = sem("o_out")

        block = ctx.enter_context(nc.Block())

        DOWNS, UPS = 4, 5
        OUTS = 8
        FILLS = 6

        plan = [("up", a, m, g) for a in range(2) for m in range(MB) for g in range(2)]
        plan += [("h1", a, m, 0) for a in range(2) for m in range(MB)]
        plan += [("h2", a, m, 0) for a in range(2) for m in range(MB)]
        plan += [("down", a, 0, 0) for a in range(2)]
        reader = []
        count = {"act": 0, "dve": 0}
        for stage, a, m, g in plan:
            e = "dve" if (stage, g) == ("up", 1) else "act"
            count[e] += 1
            reader.append((e, count[e]))
        N_MM, N_ACT, N_DVE = len(plan), count["act"], count["dve"]
        N_G = 3 * 2 * MB
        N_GH = 2 * 2 * MB

        def g_count(stage, a, m):
            return {"up": 0, "h1": 2 * MB, "h2": 4 * MB}[stage] + a * MB + m + 1

        def wait(eng, semaphore, value):
            if not isinstance(value, int) or value > 0:
                eng.wait_ge(semaphore, value)

        def quads(eng, step, tail):
            for s in range(EDGE):
                step(0, s)
            with eng.Fori(0, NQ - 1) as q:
                for s in range(EDGE, NSTEP):
                    step(q, s)
                for s in range(EDGE):
                    step(q + 1, s)
            for s in range(EDGE, NSTEP):
                step(NQ - 1, s)
            tail()

        @block.sync
        def _(sp):
            x_t = x.rearrange("o (t n p) d -> t p (o n) d", t=NT, p=128)

            def load_x(t):
                sp.dma_start(x_sb[:, NB * t:NB * (t + 1), :], x_t[t]).then_inc(x_in[t], 16)

            def load_table(t):
                sp.dma_start(tab[:, t, :, :], table[:, :, t * TILE:(t + 1) * TILE].rearrange("g p n -> p g n")).then_inc(tab_in[t], 16)

            load_x(0)
            sp.dma_start(id_sb[:], ident).then_inc(id_in, 16)
            sp.dma_start(wd_sb[:], wdown).then_inc(wd_in, 16)
            sp.dma_start(up_raw[:], wup).then_inc(up_in, 16)
            load_x(1)
            load_table(0)
            load_x(2)
            load_x(3)
            for t in range(1, NT):
                load_table(t)
            sp.dma_start(msk[:], mask).then_inc(late_in, 16)
            sp.dma_start(wo_sb[:], wo).then_inc(late_in, 16)
            sp.dma_start(sc_sb[:], scales).then_inc(late_in, 16)

            def load_q(quad, t):
                for j in range(4):
                    src = q_dram[bass.ds(quad * 4 + j, 1), :, :, t * TILE:(t + 1) * TILE]
                    src = src.rearrange("o i d n -> (o i d) n").unsqueeze(1).to_broadcast([PARTS * DQK, PARTS, TILE])
                    sp.dma_start(q_st[:, j, t * TILE:(t + 1) * TILE], src).then_inc(q_in[t], 16)

            def load_k(quad, t):
                for i in range(PARTS):
                    src = k_dram[bass.ds(quad * 4 * DH, 4 * DH), :, t * TILE:(t + 1) * TILE]
                    sp.dma_start(k_st[i * PARTS * DQK:i * PARTS * DQK + PARTS * DH, :, t * TILE:(t + 1) * TILE],
                                 src.rearrange("(h d) j n -> (d j) h n", h=4)).then_inc(k_in[t], 16)

            def load_k_rope(t):
                for i in range(PARTS):
                    src = kr_dram[:, :, t * TILE:(t + 1) * TILE].rearrange("d j n -> (d j) n")
                    sp.dma_start(k_st[i * PARTS * DQK + PARTS * DH:(i + 1) * PARTS * DQK, :, t * TILE:(t + 1) * TILE],
                                 src.unsqueeze(1).to_broadcast([PARTS * DR, 4, TILE])).then_inc(k_in[t], 16)

            def load_first(t):
                sp.wait_ge(parts_out[t], 16 * OUTS)
                load_k_rope(t)
                load_k(0, t)
                load_q(0, t)

            for t in range(NT):
                cols = slice(t * TILE, (t + 1) * TILE)
                sp.wait_ge(part2[0], t + 1)
                for i in range(PARTS):
                    sp.dma_start(q_dram[:, i, 0:DH, cols], parts[0][t % 2][:, i, :]).then_inc(parts_out[t], 16)
                sp.wait_ge(part2[1], t + 1)
                sp.dma_start(k_dram[:, :, cols], parts[1][t % 2][:]).then_inc(parts_out[t], 16)
                sp.wait_ge(part2[2], t + 1)
                for i in range(PARTS):
                    sp.dma_start(q_dram[:, i, DH:DQK, cols], parts[2][t % 2][0:64, i, :]).then_inc(parts_out[t], 16)
                sp.dma_start(kr_dram[:, :, cols], parts[2][t % 2][64:64 + DR, :, :]).then_inc(parts_out[t], 16)
                if t == 1:
                    load_first(0)
            for t in range(1, NT):
                load_first(t)
            sp.dma_start(w_raw[:, 0:2 * HID].rearrange("p (g m) -> p g m", g=2), w12.rearrange("g p m -> p g m")).then_inc(ffnw_in[0], 16)
            sp.dma_start(w_raw[:, 2 * HID:2 * HID + MB * D].rearrange("p (k m) -> p k m", k=MB),
                         w3.rearrange("(k p) m -> p k m", p=128)).then_inc(ffnw_in[0], 16)
            sp.wait_ge(ffnw_split, 4)
            sp.dma_start(w_raw[:, :].rearrange("p (g k m) -> p g k m", g=2, k=MB),
                         h12.rearrange("g (k p) m -> p g k m", p=128)).then_inc(ffnw_in[1], 16)
            with sp.Fori(0, NQ - 1) as q:
                for t in range(NT - 1):
                    sp.wait_ge(scores_done, q * (2 * NSTEP) + 2 * LAST[t])
                    load_q(q + 1, t)
                for c in range(NT):
                    sp.wait_ge(scores_done, q * (2 * NSTEP) + 2 * (LAST[NT - 2] + NB * (c + 1)))
                    load_k(q + 1, c)
                load_q(q + 1, NT - 1)

            with sp.Fori(0, NT // 2) as u:
                for a in range(2):
                    sp.wait_ge(o_ready, u * 2 + a + 3)
                    sp.dma_start(out.rearrange("o (n p) d -> p (o n) d", p=128)[:, bass.ds((u * 2 + a) * NB, NB), :],
                                 x1[:, bass.ds((u * 2 + a) * NB, NB), :]).then_inc(o_out, 16)
            sp.wait_ge(o_out, 16 * NT)

        @block.gpsimd
        def _(pool):
            pool.memset(neg_half[:], -0.5).then_inc(filled, 1)
            pool.memset(v_all[:], 1.0).then_inc(filled, 1)
            pool.memset(zeros[:], 0.0).then_inc(filled, 1)
            pool.memset(ones_col[:], 1.0).then_inc(filled, 1)
            pool.wait_ge(filled, 4)

            def inverse_root(nth, slot):
                pool.wait_ge(var_ready, nth + 1)
                pool.tensor_tensor(rstd[:, slot, :], var_eps[:, slot, :], neg_half[:], ALU.pow).then_inc(rstd_ready, 1)

            def last_part(n, t):
                pool.wait_ge(part1[n], t + 1)
                pool.tensor_tensor(parts[n][t % 2][:, 2, :], resid[n][t % 2][:], parts[n][t % 2][:, 1, :],
                                   ALU.subtract).then_inc(part2[n], 1)

            inverse_root(0, 0)
            inverse_root(1, 1)
            for t in range(NT):
                if t + 2 < NT:
                    inverse_root(t + 2, t + 2)
                pool.wait_ge(rope_mul, t + 1)
                wait(pool, resid0[2], t)
                pool.tensor_tensor(rope[2][:], rope[0][:], rope[1][:], ALU.add).then_inc(rope_done, 1)
                for n in range(3):
                    last_part(n, t)

            def v_stage(quad, c):
                return pool.tensor_tensor(v_quad[:, NB * c:NB * (c + 1), :, :].rearrange("p k h v -> p k (h v)"),
                                          v_all[:, NB * c:NB * (c + 1), bass.ds(quad, 1), :].rearrange("p k o v -> p k (o v)"),
                                          zeros[:].rearrange("p (k v) -> p k v", k=NB), ALU.add)

            pool.wait_ge(v_copied, NT)
            for c in range(NT):
                v_stage(0, c).then_inc(v_in, 1)

            raw12 = w_raw[:, 0:2 * HID].rearrange("p (g m) -> p g m", g=2)
            raw3 = w_raw[:, 2 * HID:2 * HID + MB * D].rearrange("p (k m) -> p k m", k=MB)
            rawh = w_raw[:, :].rearrange("p (g k m) -> p g k m", g=2, k=MB)
            pool.wait_ge(ffnw_in[0], 32)
            pool.tensor_copy(w12h[:], raw12).then_inc(ffnw_split, 1)
            pool.tensor_copy(w3h[:], raw3).then_inc(ffnw_split, 1)
            pool.wait_ge(ffnw_split, 2)
            pool.tensor_tensor(w12l[:], raw12, w12h[:].bitcast(F32), ALU.subtract).then_inc(ffnw_split, 1)
            pool.tensor_tensor(w3l[:], raw3, w3h[:].bitcast(F32), ALU.subtract).then_inc(ffnw_split, 1)
            pool.wait_ge(ffnw_in[1], 16)
            pool.tensor_copy(h12h[:], rawh).then_inc(ffnw_split, 1)
            pool.wait_ge(ffnw_split, 5)
            pool.tensor_tensor(h12l[:], rawh, h12h[:].bitcast(F32), ALU.subtract).then_inc(ffnw_split, 1)

            with pool.Fori(0, NQ - 1) as q:
                for c in range(NT):
                    pool.wait_ge(pv_done, q * NSTEP + (LAST[NT - 2] + NB * (c + 1)))
                    v_stage(q + 1, c).then_inc(v_in, 1)

            def add_x1(t):
                pool.wait_ge(yb_ready, t + 1)
                pool.tensor_tensor(x1[:, NB * t:NB * (t + 1), :], x_sb[:, NB * t:NB * (t + 1), :], yb[:, t % 2, :, :], ALU.add).then_inc(x1_ready, 1)

            for nth, what in enumerate(LN2_ORDER):
                stage, t = what
                if (stage, t % 2) == ("ffn", 0):
                    add_x1(t)
                    add_x1(t + 1)
                inverse_root(NT + nth, (NT + nth) % LNB)

            pool.sem_inc(o_ready, 2)
            with pool.Fori(0, NT // 2) as u:
                for a in range(2):
                    tile = u * 2 + a
                    inverse_root(3 * NT + tile, a)
                    pool.wait_ge(yb_ready, NT + tile + 1)
                    o = x1[:, bass.ds(tile * NB, NB), :]
                    pool.tensor_tensor(o, o, yb[:, a, :, :], ALU.add).then_inc(o_ready, 1)

        @block.scalar
        def _(act):
            def rope_part(n, t):
                if n == 0:
                    act.wait_ge(rope_done, t + 1)
                    act.activation(parts[2][t % 2][:, 0, :], rope[2][:], ACT.Copy).then_inc(part0[2], 1)
                else:
                    second_part(2, t)

            def second_part(n, t):
                act.wait_ge(resid0[n], t + 1)
                act.activation(parts[n][t % 2][:, 1, :], resid[n][t % 2][:], ACT.Copy).then_inc(part1[n], 1)

            for t in range(NT):
                act.wait_ge(tr_done, t + 1)
                wait(act, down_done, DOWNS * (t - 1))
                act.activation(xnT[:, t % 2, :], ps[:, B_TR, :], ACT.Copy).then_inc(xnT_ready, 1)
                for i in range(2):
                    act.wait_ge(down_done, DOWNS * t + i + 1)
                    wait(act, up_done, UPS * t)
                    act.activation(c_sb[i][:], ps[:, B_C + i, :], ACT.Copy).then_inc(c_hi, 1)
                    if t > 0:
                        rope_part(i, t - 1)
                if t > 1:
                    act.wait_ge(parts_out[t - 2], 16 * OUTS)
                for n in range(2):
                    act.wait_ge(up_done, UPS * t + (1, 4)[n])
                    act.activation(parts[n][t % 2][:, 0, :], ps[:, (B_QC, B_KC)[n], :], ACT.Copy).then_inc(part0[n], 1)
                act.wait_ge(up_done, UPS * t + 5)
                act.wait_ge(filled, 2)
                act.activation(v_all[:, NB * t:NB * (t + 1), :, :].rearrange("p n q (h v) -> p n (q h) v", v=VW)[:, :, :, 0:DH],
                               ps[:, B_V, :].rearrange("p (n h v) -> p n h v", n=NB, v=DH), ACT.Copy).then_inc(v_copied, 1)
                for n in range(2):
                    second_part(n, t)
            rope_part(0, NT - 1)
            rope_part(1, NT - 1)

            act.wait_ge(rope_mul, NT)
            act.wait_ge(up_done, UPS * NT)

            def exps(q, s):
                t, kb, c0 = STEPS[s]
                wait(act, pv_done, q * NSTEP + (s - PBUF + 1))
                for half in range(2):
                    h = 2 * s + half
                    act.wait_ge(scores_done, q * (2 * NSTEP) + (h + 1))
                    slot = 2 * SLOT[h]
                    act.activation(p_sb[:, s % PBUF, 2 * half:2 * half + 2, c0:], ps[:, slot:slot + 2, c0:],
                                   ACT.Exp, scale=SCALE).then_inc(exp_done, 1)

            quads(act, exps, lambda: None)

            def copy_attnT(t):
                act.wait_ge(at_done, t + 1)
                wait(act, wo_done, t - 1)
                act.activation(attnT[:, t % 2, :], ps[:, B_AT + t % 2, :], ACT.Copy).then_inc(attnT_ready, 1)

            def apply_ln(dst, src, slot):
                for n in range(NB):
                    i = act.activation(dst[:, n, :], src[:, n * D:(n + 1) * D], ACT.Identity, bias=nb[:, slot, n:n + 1], scale=rstd[:, slot, n:n + 1])
                return i

            def normalise_attn(t):
                act.wait_ge(nb_ready, t + 1)
                wait(act, x1_ready, t - 1)
                apply_ln(yb[:, t % 2], ps[:, B_WO + t, :], LN2_SLOT["att", t]).then_inc(yb_ready, 1)

            def ffn_input_hi(t):
                act.wait_ge(t2_done, t + 1)
                act.activation(xTh[:, t * TILE:(t + 1) * TILE], ps[:, B_T2 + t % 2, :], ACT.Copy).then_inc(xTh_ready, 1)

            for t in range(NT):
                copy_attnT(t)
            for t in (0, 2):
                normalise_attn(t)
                normalise_attn(t + 1)
                ffn_input_hi(t)
                ffn_input_hi(t + 1)

            act.sem_inc(ff_act, 1)
            act.wait_ge(late_in, 48)
            with act.Fori(0, NT // 2) as u:
                n_s = n_g = 0
                for o, (stage, a, m, g) in enumerate(plan):
                    bank = o % FF_BANKS
                    if (stage, g) == ("up", 1):
                        continue
                    act.wait_ge(ff_mm, u * N_MM + (o + 1))
                    if stage == "up":
                        act.wait_ge(ff_dve, u * N_DVE + (1 + max(0, n_s - 1)))
                        act.activation(s_f[n_s % 2][:], ps[:, bank, :], ACT.Silu, scale=sc_sb[:, m:m + 1]).then_inc(ff_act, 1)
                        n_s += 1
                    elif stage == "down":
                        act.activation(y_sb[a][:], ps[:, bank, :], ACT.Copy, scale=sc_sb[:, 4 * MB:4 * MB + 1]).then_inc(ff_act, 1)
                    else:
                        k = {"h1": 2, "h2": 3}[stage]
                        gen = {"h1": 1, "h2": 0}[stage]
                        act.wait_ge(g_ready, u * N_G + (2 * MB + max(0, n_g - 2)))
                        act.activation(g_f[n_g % 3][:], ps[:, bank, :], ACT.Gelu, scale=sc_sb[:, k * MB + m:k * MB + m + 1])
                        act.activation(g_h[gen][a][:, m, :], ps[:, bank, :], ACT.Gelu, scale=sc_sb[:, k * MB + m:k * MB + m + 1]).then_inc(ff_act, 1)
                        n_g += 1
                for a in range(2):
                    tile = u * 2 + a
                    act.wait_ge(nb_ready, NT + tile + 1)
                    act.wait_ge(o_ready, u * 2 + (a + 1))
                    apply_ln(yb[:, a], ps[:, B_YT + a, :], a).then_inc(yb_ready, 1)

        @block.vector
        def _(dve):
            def stats(src, nth, slot):
                for n in range(NB):
                    i = dve.bn_stats(stat[:, slot, n, :], src(n))
                i.then_inc(stats_done, 1)
                dve.wait_ge(stats_done, nth + 1)
                if not isinstance(nth, int):
                    dve.sem_inc(stats_seen, 1)
                for n in range(NB):
                    i = dve.bn_aggr(mv[:, slot, n, :], stat[:, slot, n, :])
                i.then_inc(mv_done, 1)
                dve.wait_ge(mv_done, nth + 1)
                dve.tensor_scalar(var_eps[:, slot, :], mv[:, slot, :, 1], EPS, None, ALU.add).then_inc(var_ready, 1)

            def apply_x(dst, src, nth, slot):
                dve.wait_ge(rstd_ready, nth + 1)
                for n in range(NB):
                    i = dve.tensor_scalar(dst(n), src(n), mv[:, slot, n, 0:1], rstd[:, slot, n:n + 1], ALU.subtract, ALU.mult)
                return i

            def stats_x(t):
                dve.wait_ge(x_in[t], 16)
                stats(lambda n: x_sb[:, NB * t + n, :], t, t)

            def norm_x(t):
                apply_x(lambda n: xn[:, NB * t + n, :], lambda n: x_sb[:, NB * t + n, :], t, t).then_inc(xn_ready, 1)

            def split_up_weights():
                dve.wait_ge(up_in, 16)
                dve.tensor_copy(up_sb[:], up_raw[:]).then_inc(up_split, 1)
                dve.wait_ge(up_split, 1)
                for g in (1, 3):
                    r = slice(32 * g, 32 * g + 32)
                    dve.tensor_tensor(up_sb[r, :], up_raw[r, :], up_sb[r, :].bitcast(F32), ALU.subtract).then_inc(up_split, 1)

            def residual(n, t):
                dve.wait_ge(part0[n], t + 1)
                wait(dve, part2[n], t - 1)
                src = ps[:, (B_QC, B_KC)[n], :] if n < 2 else rope[2][:]
                dve.tensor_tensor(resid[n][t % 2][:], src, parts[n][t % 2][:, 0, :], ALU.subtract).then_inc(resid0[n], 1)

            stats_x(0)
            stats_x(1)
            norm_x(0)
            split_up_weights()
            norm_x(1)
            for t in range(NT):
                for i in range(2):
                    dve.wait_ge(c_hi, t * 2 + i + 1)
                    dve.tensor_tensor(c_sb[i][64:128, :], ps[64:128, B_C + i, :], c_sb[i][64:128, :].bitcast(F32),
                                      ALU.subtract).then_inc(c_lo, 1)
                if t > 0:
                    residual(2, t - 1)
                if t + 2 < NT:
                    stats_x(t + 2)
                dve.wait_ge(tab_in[t], 16)
                dve.wait_ge(down_done, DOWNS * t + 4)
                dve.wait_ge(up_done, UPS * t + 3)
                wait(dve, rope_done, t)
                dve.tensor_tensor(rope[0][:], ps[:, B_RA, :], tab[:, t, 0, :], ALU.mult)
                dve.tensor_tensor(rope[1][:], ps[:, B_RB, :], tab[:, t, 1, :], ALU.mult).then_inc(rope_mul, 1)
                residual(0, t)
                residual(1, t)
                if t + 2 < NT:
                    norm_x(t + 2)
            residual(2, NT - 1)

            dve.wait_ge(v_copied, NT)
            dve.wait_ge(resid0[1], NT)
            dve.memset(ps[:, B_ACC:B_ACC + 2, :], 0.0).then_inc(acc_zero, 1)
            dve.wait_ge(late_in, 48)

            def clip(q, s, half):
                t, kb, c0 = STEPS[s]
                dve.wait_ge(exp_done, q * (2 * NSTEP) + (2 * s + half + 1))
                p = p_sb[:, s % PBUF, 2 * half:2 * half + 2, :]
                if kb < NB * t:
                    i = dve.tensor_scalar(p, p, LO, HI, ALU.max, ALU.min)
                else:
                    d = p[:, :, c0:c0 + 128]
                    i = dve.scalar_tensor_tensor(d, d, LO, msk[:].unsqueeze(1).to_broadcast([128, 2, 128]), ALU.max, ALU.min)
                    if c0 + 128 < TILE:
                        r = p[:, :, c0 + 128:]
                        i = dve.tensor_scalar(r, r, LO, HI, ALU.max, ALU.min)
                i.then_inc(clip_done, 1)

            def evacuate(q, t):
                dve.wait_ge(pv_done, q * NSTEP + LAST[t])
                wait(dve, accT_done, q * NT + t)
                dve.tensor_copy(acc_sb[:], ps[:, B_ACC + t % 2, :]).then_inc(acc_out, 1)

            def normalise(q, t):
                dve.wait_ge(accT_done, q * NT + (t + 1))
                bank = ps[:, B_ACC + t % 2, :].rearrange("p (n h v) -> p n h v", n=NB, h=4)
                dve.reciprocal(rcp[:], bank[:, :, :, DH]).then_inc(rcp_done, 1)
                dve.wait_ge(rcp_done, q * NT + (t + 1))
                dst = attn[:, NB * t:NB * (t + 1), bass.ds(q * (4 * DH), 4 * DH)].rearrange("p n (h v) -> p n h v", h=4)
                dve.tensor_tensor(dst, bank[:, :, :, 0:DH], rcp[:].unsqueeze(3).to_broadcast([128, NB, 4, DH]), ALU.mult).then_inc(attn_done, 1)

            def lo_of_weights():
                dve.wait_ge(ffnw_split, 6)
                pieces = [w12l[:, 0, :], w12l[:, 1, :], w3l[:].rearrange("p k m -> p (k m)")]
                pieces += [h12l[:, g, :, :].rearrange("p k m -> p (k m)") for g in range(2)]
                for n, w in enumerate(pieces):
                    i = dve.tensor_reduce(lo_max[:, n:n + 1], w.bitcast(F32), mybir.AxisListType.X, ALU.max, apply_absolute_value=True)
                i.then_inc(lo_step, 1)
                dve.wait_ge(lo_step, 1)
                dve.tensor_reduce(lo_max[:, 5:6], lo_max[:, 0:5], mybir.AxisListType.X, ALU.max).then_inc(lo_step, 1)
                dve.wait_ge(lo_step, 2)
                dve.tensor_scalar(lo_any[:], lo_max[:, 5:6], 0.0, None, ALU.is_gt).then_inc(lo_step, 1)

            def vector_step(q, s):
                t, kb, c0 = STEPS[s]
                for half in range(2):
                    clip(q, s, half)
                prev = isinstance(q, int) and q == 0
                if s == 2 and not prev:
                    evacuate(q - 1, NT - 1)
                if s == 5 and not prev:
                    normalise(q - 1, NT - 1)
                if t > 0 and kb == 2:
                    evacuate(q, t - 1)
                if t > 0 and kb == 6:
                    normalise(q, t - 1)

            def vector_tail():
                evacuate(NQ - 1, NT - 1)
                normalise(NQ - 1, NT - 1)

            quads(dve, vector_step, vector_tail)

            def minus_mean(nth, slot):
                dve.wait_ge(rstd_ready, nth + 1)
                dve.scalar_tensor_tensor(nb[:, slot, :], mv[:, slot, :, 0], -1.0, rstd[:, slot, :], ALU.mult, ALU.mult).then_inc(nb_ready, 1)

            def stats_att(t):
                dve.wait_ge(wo_done, t + 1)
                stats(lambda n: ps[:, B_WO + t, n * D:(n + 1) * D], LN2_NTH["att", t], LN2_SLOT["att", t])

            def stats_ffn(t):
                dve.wait_ge(x1_ready, t + 1)
                stats(lambda n: x1[:, t * NB + n, :], LN2_NTH["ffn", t], LN2_SLOT["ffn", t])

            def norm_ffn(t):
                wait(dve, t2_done, t - 1)
                apply_x(lambda n: xn2[:, t % 2, n, :], lambda n: x1[:, t * NB + n, :], LN2_NTH["ffn", t], LN2_SLOT["ffn", t]).then_inc(xn2_ready, 1)

            def ffn_input_lo(t):
                dve.wait_ge(xTh_ready, t + 1)
                cols = slice(t * TILE, (t + 1) * TILE)
                dve.tensor_tensor(xTl[:, cols], ps[:, B_T2 + t % 2, :], xTh[:, cols].bitcast(F32), ALU.subtract).then_inc(xTl_ready, 1)

            stats_att(0)
            stats_att(1)
            minus_mean(LN2_NTH["att", 0], LN2_SLOT["att", 0])
            minus_mean(LN2_NTH["att", 1], LN2_SLOT["att", 1])
            stats_ffn(0)
            stats_ffn(1)
            lo_of_weights()
            norm_ffn(0)
            norm_ffn(1)
            stats_att(2)
            stats_att(3)
            ffn_input_lo(0)
            ffn_input_lo(1)
            minus_mean(LN2_NTH["att", 2], LN2_SLOT["att", 2])
            minus_mean(LN2_NTH["att", 3], LN2_SLOT["att", 3])
            stats_ffn(2)
            stats_ffn(3)
            norm_ffn(2)
            norm_ffn(3)
            ffn_input_lo(2)
            ffn_input_lo(3)
            dve.wait_ge(flag_mm, 1)
            dve.tensor_copy(lo_flag[:], ps[0:1, B_AT, 0:1]).then_inc(flag_ready, 1)

            dve.sem_inc(ff_dve, 1)
            with dve.Fori(0, NT // 2) as u:
                n_g = n_u = 0
                for o, (stage, a, m, g) in enumerate(plan):
                    bank = o % FF_BANKS
                    if (stage, g) == ("up", 1):
                        full = u_f[n_u % 2]
                        dve.wait_ge(ff_mm, u * N_MM + (o + 1))
                        dve.wait_ge(ff_act, u * N_ACT + (1 + reader[o - 1][1]))
                        dve.scalar_tensor_tensor(full[:], ps[:, bank, :], sc_sb[:, MB + m:MB + m + 1], s_f[n_u % 2][:],
                                                 ALU.mult, ALU.mult).then_inc(ff_dve, 1)
                        n_u += 1
                        dve.wait_ge(ff_dve, u * N_DVE + (1 + n_u))
                        dve.tensor_copy(g_h[0][a][:, m, :], full[:]).then_inc(uh_ready, 1)
                        dve.wait_ge(uh_ready, u * N_DVE + n_u)
                        dve.tensor_tensor(g_l[0][a][:, m, :], full[:], g_h[0][a][:, m, :].bitcast(F32), ALU.subtract).then_inc(g_ready, 1)
                    elif stage in ("h1", "h2"):
                        gen = {"h1": 1, "h2": 0}[stage]
                        dve.wait_ge(ff_act, u * N_ACT + (1 + reader[o][1]))
                        dve.tensor_tensor(g_l[gen][a][:, m, :], g_f[n_g % 3][:], g_h[gen][a][:, m, :].bitcast(F32), ALU.subtract).then_inc(g_ready, 1)
                        n_g += 1
                    elif stage == "down":
                        tile = u * 2 + a
                        dve.wait_ge(yT_done, tile + 1)
                        stats(lambda n: ps[:, B_YT + a, n * D:(n + 1) * D], 3 * NT + tile, a)
                        minus_mean(3 * NT + tile, a)

        @block.tensor
        def _(pe):
            def transpose4(bank, src):
                for n in range(NB):
                    i = pe.transpose(ps[:, bank, n * 128:(n + 1) * 128], src(n), id_sb[:])
                return i

            def turn_x(t):
                pe.wait_ge(xn_ready, t + 1)
                wait(pe, xnT_ready, t)
                transpose4(B_TR, lambda n: xn[:, NB * t + n, :]).then_inc(tr_done, 1)

            pe.wait_ge(id_in, 16)
            turn_x(0)
            pe.wait_ge(wd_in, 16)
            for t in range(NT):
                pe.wait_ge(xnT_ready, t + 1)
                wait(pe, c_lo, t * 2)
                for i in range(2):
                    pe.matmul(ps[:, B_C + i, :], wd_sb[:, i * 128:(i + 1) * 128], xnT[:, t % 2, :], start=True, stop=True).then_inc(down_done, 1)
                wait(pe, rope_mul, t)
                for i in range(2):
                    pe.matmul(ps[64:128, B_RA + i, :], wd_sb[:, 256 + i * 64:256 + (i + 1) * 64], xnT[:, t % 2, :],
                              start=True, stop=True).then_inc(down_done, 1)
                if t + 1 < NT:
                    turn_x(t + 1)
                pe.wait_ge(up_split, 3)
                pe.wait_ge(c_lo, t * 2 + 1)
                wait(pe, resid0[0], t)
                pe.matmul(ps[:, B_QC, :], up_sb[:, 0:128], c_sb[0][:], start=True, stop=True).then_inc(up_done, 1)
                for i in range(2):
                    pe.matmul(ps[0:64, B_RA + i, :], up_sb[:, 128 + i * 64:128 + (i + 1) * 64], c_sb[0][:],
                              start=True, stop=True).then_inc(up_done, 1)
                pe.wait_ge(c_lo, t * 2 + 2)
                wait(pe, resid0[1], t)
                pe.matmul(ps[:, B_KC, :], up_sb[:, 256:384], c_sb[1][:], start=True, stop=True).then_inc(up_done, 1)
                wait(pe, v_copied, t)
                for n in range(NB):
                    i = pe.matmul(ps[:, B_V, n * 128:(n + 1) * 128], c_sb[1][:, n * 128:(n + 1) * 128], up_sb[:, 384:512], start=True, stop=True)
                i.then_inc(up_done, 1)

            def scores(q, h):
                s, half = h // 2, h % 2
                t, kb, c0 = STEPS[s]
                if kb == 0 and half == 0:
                    pe.wait_ge(q_in[t], (q + 1) * (16 * 4))
                if kb == NB * t and half == 0:
                    pe.wait_ge(k_in[t], (q + 2) * (16 * PARTS))
                wait(pe, exp_done, q * (2 * NSTEP) + SLOT_USED[h])
                for j in range(2):
                    i = pe.matmul(ps[:, 2 * SLOT[h] + j, c0:], k_st[:, 2 * half + j, kb * 128:(kb + 1) * 128],
                                  q_st[:, 2 * half + j, t * TILE + c0:(t + 1) * TILE], start=True, stop=True)
                i.then_inc(scores_done, 1)

            def weigh(q, s):
                t, kb, c0 = STEPS[s]
                pe.wait_ge(clip_done, q * (2 * NSTEP) + (2 * s + 2))
                if kb == NB * t:
                    pe.wait_ge(v_in, q * NT + (t + 1))
                if kb == 0:
                    wait(pe, attn_done, q * NT + (t - 1))
                for j in range(4):
                    i = pe.matmul(ps[32 * j:32 * j + VW, B_ACC + t % 2, c0:], v_quad[:, kb, j, :], p_sb[:, s % PBUF, j, c0:],
                                  start=(kb == 0), stop=(kb == NB * (t + 1) - 1))
                i.then_inc(pv_done, 1)

            def turn(q, t):
                pe.wait_ge(acc_out, q * NT + (t + 1))
                transpose4(B_ACC + t % 2, lambda n: acc_sb[:, n * 128:(n + 1) * 128]).then_inc(accT_done, 1)

            def tensor_step(q, s):
                first = isinstance(q, int) and q == 0
                scores(q, 2 * s)
                scores(q, 2 * s + 1)
                if s >= LAG:
                    weigh(q, s - LAG)
                elif not first:
                    weigh(q - 1, NSTEP + s - LAG)
                t, kb, _ = STEPS[s]
                if s == 5 and not first:
                    turn(q - 1, NT - 1)
                if t > 0 and kb == 5:
                    turn(q, t - 1)

            def tensor_tail():
                for s in range(NSTEP - LAG, NSTEP):
                    weigh(NQ - 1, s)
                turn(NQ - 1, NT - 1)

            pe.wait_ge(xnT_ready, NT)
            pe.wait_ge(c_lo, 2 * NT)
            pe.wait_ge(rope_mul, NT)
            pe.wait_ge(resid0[0], NT)
            pe.wait_ge(acc_zero, 1)
            quads(pe, tensor_step, tensor_tail)

            pe.wait_ge(attn_done, NQ * NT)
            for t in range(NT):
                wait(pe, attnT_ready, t - 1)
                transpose4(B_AT + t % 2, lambda n: attn[:, t * NB + n, :]).then_inc(at_done, 1)
                if t == 0:
                    pe.wait_ge(late_in, 48)
                pe.wait_ge(attnT_ready, t + 1)
                for n in range(NB):
                    i = pe.matmul(ps[:, B_WO + t, n * D:(n + 1) * D], attnT[:, t % 2, n * 128:(n + 1) * 128], wo_sb[:], start=True, stop=True)
                i.then_inc(wo_done, 1)
            pe.wait_ge(lo_step, 3)
            pe.matmul(ps[0:1, B_AT, 0:1], lo_any[:], ones_col[:], start=True, stop=True).then_inc(flag_mm, 1)
            for t in range(NT):
                pe.wait_ge(xn2_ready, t + 1)
                wait(pe, xTl_ready, t - 1)
                transpose4(B_T2 + t % 2, lambda n: xn2[:, t % 2, n, :]).then_inc(t2_done, 1)

            def product(bank, terms, with_lo):
                n, last = 0, (4 if with_lo else 2) * len(terms) - 1
                for ready, wh, wl, ah, al in terms:
                    if ready is not None:
                        pe.wait_ge(g_ready, ready)
                    for w, v in ((wh, ah), (wh, al), (wl, ah), (wl, al))[:4 if with_lo else 2]:
                        i = pe.matmul(ps[:, bank, :], w, v, start=(n == 0), stop=(n == last))
                        n += 1
                i.then_inc(ff_mm, 1)

            def ffn_pairs(with_lo):
                with pe.Fori(0, NT // 2) as u:
                    for o, (stage, a, m, g) in enumerate(plan):
                        bank = o % FF_BANKS
                        if o < FF_BANKS:
                            pe.wait_ge(ff_act, u * N_ACT + 1)
                            pe.wait_ge(ff_dve, u * N_DVE + 1)
                        else:
                            engine, n = reader[o - FF_BANKS]
                            if engine == "act":
                                pe.wait_ge(ff_act, u * N_ACT + (1 + n))
                            else:
                                pe.wait_ge(ff_dve, u * N_DVE + (1 + n))
                        cols = slice(m * 128, (m + 1) * 128)
                        if stage == "up":
                            tok = bass.ds((u * 2 + a) * TILE, TILE)
                            terms = [(None, w12h[:, g, cols], w12l[:, g, cols], xTh[:, tok], xTl[:, tok])]
                        elif stage == "h1":
                            terms = [(u * N_G + g_count("up", a, k), h12h[:, 0, k, cols], h12l[:, 0, k, cols],
                                      g_h[0][a][:, k, :], g_l[0][a][:, k, :]) for k in range(MB)]
                        elif stage == "h2":
                            terms = [(u * N_G + g_count("h1", a, k), h12h[:, 1, k, cols], h12l[:, 1, k, cols],
                                      g_h[1][a][:, k, :], g_l[1][a][:, k, :]) for k in range(MB)]
                        else:
                            terms = [(u * N_G + g_count("h2", a, k), w3h[:, k, :], w3l[:, k, :],
                                      g_h[0][a][:, k, :], g_l[0][a][:, k, :]) for k in range(MB)]
                        product(bank, terms, with_lo)
                    for a in range(2):
                        pe.wait_ge(ff_act, u * N_ACT + (1 + reader[N_MM - 2 + a][1]))
                        pe.wait_ge(yb_ready, NT + u * 2)
                        transpose4(B_YT + a, lambda n: y_sb[a][:, n * 128:(n + 1) * 128]).then_inc(yT_done, 1)

            pe.wait_ge(flag_ready, 1)
            pe.wait_ge(xTl_ready, NT)
            flag = pe.value_load(lo_flag[0:1, 0:1].bitcast(mybir.dt.int32))
            with pe.If(flag != 0):
                ffn_pairs(True)
            with pe.Else():
                ffn_pairs(False)


def kernel(L0_attn_x, L0_attn_W_DQ, L0_attn_W_UQ, L0_attn_W_QR, L0_attn_W_DKV, L0_attn_W_UK, L0_attn_W_UV,
           L0_attn_W_KR, L0_attn_W_O, L0_ffn_w1_w, L0_ffn_w1_s, L0_ffn_w2_w, L0_ffn_w2_s, L0_ffn_h1_w, L0_ffn_h1_s,
           L0_ffn_h2_w, L0_ffn_h2_s, L0_ffn_w3_w, L0_ffn_w3_s):
    import concourse.bacc as bacc
    from concourse.bass_utils import run_bass_kernel_spmd

    a = np.asarray
    swap = np.arange(H * DR) ^ 1
    kr = np.tile(a(L0_attn_W_KR), (1, H))
    wup = np.concatenate([a(L0_attn_W_UQ), a(L0_attn_W_QR), a(L0_attn_W_QR)[:, swap], a(L0_attn_W_UK), a(L0_attn_W_UV)], axis=1)
    inv = np.float32(10000.0) ** (-np.arange(0, DR, 2, dtype=np.float32) / np.float32(DR))
    angle = (np.arange(S, dtype=np.float32)[:, None] * inv).T.astype(np.float64)
    cos = np.repeat(np.cos(angle), 2, axis=0)
    sin = np.repeat(np.sin(angle), 2, axis=0) * np.array([-1.0, 1.0, -1.0, 1.0])[:, None]
    arrays = {
        "x": a(L0_attn_x),
        "wdown": np.concatenate([np.tile(a(L0_attn_W_DQ), (1, 4)), np.tile(a(L0_attn_W_DKV), (1, 4)), kr, kr[:, swap]], axis=1),
        "wup": np.tile(wup, (4, 1)),
        "table": np.stack([np.tile(cos, (2 * H, 1)), np.tile(sin, (2 * H, 1))]).astype(np.float32),
        "ident": np.eye(128, dtype=np.float32),
        "mask": np.where(np.arange(128)[None, :] >= np.arange(128)[:, None], np.float32(HI), np.float32(0)),
        "wo": a(L0_attn_W_O),
        "w12": np.stack([a(L0_ffn_w1_w).T, a(L0_ffn_w2_w).T]),
        "h12": np.stack([a(L0_ffn_h1_w).T, a(L0_ffn_h2_w).T]),
        "w3": a(L0_ffn_w3_w).T,
"scales": np.concatenate([a(v).reshape(-1, 128) for v in (L0_ffn_w1_s, L0_ffn_w2_s, L0_ffn_h1_s, L0_ffn_h2_s, L0_ffn_w3_s)]).T,
    }
    nc = bacc.Bacc("TRN2", target_bir_lowering=False, num_devices=1)
    ins, args = {}, {}
    for name, v in arrays.items():
        v = np.ascontiguousarray(v)
        ins["in_" + name] = v
        args[name] = nc.dram_tensor("in_" + name, v.shape, F32, kind="ExternalInput").ap()
    args["out"] = nc.dram_tensor("out", (1, S, D), F32, kind="ExternalOutput").ap()
    build(nc, **args)
    r = run_bass_kernel_spmd(nc, [ins], core_ids=[0])
    return r.results[0]["out"]
```

```python
from contextlib import ExitStack

import numpy as np
import concourse.bass as bass
from concourse import mybir

F32 = mybir.dt.float32
F32R = mybir.dt.float32r
BF16 = mybir.dt.bfloat16
ALU = mybir.AluOpType
ACT = mybir.ActivationFunctionType

S = 2048
D = 128
H, DH, DR = 16, 8, 4
DQK = DH + DR
HID = 512
MB = HID // 128
TILE = 512
NT = S // TILE
NB = TILE // 128
KB = S // 128
NQ = H // 4
PARTS = 3
ROWS = PARTS * PARTS * DQK
VW = DH + 1
EPS = 1e-5
SCALE = 1.0 / float(np.sqrt(np.float32(DQK)))
HI = float(np.exp(80.0 * SCALE))
LO = float(np.exp(-80.0 * SCALE))
PBUF = 4
SLOTS = 3


def steps():
    out = []
    for t in range(NT):
        blocks = []
        for d in range(NB):
            blocks += [NB * t + d] + [t * d + n for n in range(t)]
        out += [(t, i, kb, max(0, kb - NB * t) * 128) for i, kb in enumerate(blocks)]
    return out


STEPS = steps()
NSTEP = len(STEPS)
KEYS_USED = [1 + max(s for s, (t, _, kb, _) in enumerate(STEPS) if t == NT - 1 and kb // NB == c) for c in range(NT)]
LAST = [NB * (t + 1) * (t + 2) // 2 for t in range(NT)]
EDGE = 7
EVACUATE, TURN, NORMALISE = 1, 3, 3
LAG = 2
SLOT = [h % SLOTS for h in range(2 * NSTEP)]
SLOT_USED = [max(u for u in range(h - 2 * NSTEP, h) if SLOT[u % (2 * NSTEP)] == SLOT[h]) + 1 for h in range(2 * NSTEP)]
LO_STEPS = (33, 35, 37)
LO_PIECES = len(LO_STEPS) * (NQ - 1)
LO_COLS = -(-(3 + 2 * MB) * HID // (LO_PIECES * 128)) * 128
LNB = 4
LN2_ORDER = [("att", 0), ("ffn", 0), ("att", 1), ("att", 2), ("ffn", 1), ("att", 3), ("ffn", 2), ("ffn", 3)]
LN2_NTH = {what: NT + n for n, what in enumerate(LN2_ORDER)}
LN2_SLOT = {what: (NT + n) % LNB for n, what in enumerate(LN2_ORDER)}

FFN_PLAN = [("h1", 1, 0), ("h1", 2, 0), ("h1", 3, 0), ("gate", 0, 1), ("up", 0, 1), ("gate", 1, 1), ("up", 1, 1), ("h2", 0, 0),
            ("gate", 2, 1), ("up", 2, 1), ("gate", 3, 1), ("up", 3, 1), ("h2", 1, 0), ("h2", 2, 0), ("h2", 3, 0),
            ("h1", 0, 1), ("down", 0, 0)]
FF_BANKS = 6


def ffn_counts():
    signals = {"mm": ("gate", "up", "h1", "h2", "down"), "act": ("gate", "h1", "h2", "down"), "dve": ("gate", "up"),
               "low": ("h1", "h2"), "u": ("up",)}
    at, total = {}, {}
    for kind, tiles in (("first", (1,)), ("mid", (0, 1)), ("last", (0,))):
        for name, stages in signals.items():
            n = 0
            for pos, (stage, m, tile) in enumerate(FFN_PLAN):
                if tile in tiles:
                    n += stage in stages
                    at[kind, name, pos] = n
            total[kind, name] = n
    return at, total


AT, TOTAL = ffn_counts()


def build(nc, x, wdown, wup, table, ident, mask, wo, w12, h12, w3, scales, out):
    with ExitStack() as ctx:
        def sb(name, shape, dt=F32, stack=ctx):
            return stack.enter_context(nc.sbuf_tensor(name, shape, dt))

        def sem(name):
            return ctx.enter_context(nc.semaphore(name))

        x_sb = sb("x_sb", [128, KB, D])
        attn = sb("attn", [128, KB, D])
        id_sb = sb("id_sb", [128, 128])
        wo_sb = sb("wo_sb", [128, D])
        sc_sb = sb("sc_sb", [128, 4 * MB + 1])
        w12h = sb("w12h", [128, 2, HID], F32R)
        h12h = sb("h12h", [128, 2, MB, HID], F32R)
        w3h = sb("w3h", [128, MB, D], F32R)
        w_lo = sb("w_lo", [128, LO_PIECES * LO_COLS], F32R)
        w12l = w_lo[:, 0:2 * HID].rearrange("p (g m) -> p g m", g=2)
        w3l = w_lo[:, 2 * HID:3 * HID].rearrange("p (k m) -> p k m", k=MB)
        h12l = w_lo[:, 3 * HID:11 * HID].rearrange("p (g k m) -> p g k m", g=2, k=MB)
        stat = sb("stat", [128, LNB, NB, 6])
        mv = sb("mv", [128, LNB, NB, 2])
        var_eps = sb("var_eps", [128, LNB, NB])
        rstd = sb("rstd", [128, LNB, NB])
        neg_half = sb("neg_half", [128, NB])
        lo_max = sb("lo_max", [128, LO_PIECES])
        lo_any = sb("lo_any", [128, 1])
        ones_col = sb("ones_col", [128, 1])
        lo_flag = sb("lo_flag", [1, 1])
        half_sc = sb("half_sc", [128, 2, MB])

        split = ExitStack()
        parts = [[sb(f"part{n}{b}", [128, PARTS, TILE], BF16, stack=split) for b in range(2)] for n in range(3)]
        resid = [[sb(f"resid{n}{b}", [128, TILE], stack=split) for b in range(2)] for n in range(3)]
        rope = [sb(f"rope{i}", [128, TILE], stack=split) for i in range(3)]
        split.close()
        x1 = sb("x1", [128, KB, D])
        yb = sb("yb", [128, 2, NB, D])
        attnT = sb("attnT", [128, TILE])
        xn2 = sb("xn2", [128, 2, NB, D])
        xTh = sb("xTh", [128, S], F32R)
        xTl = sb("xTl", [128, S], F32R)
        y_sb = sb("y_sb", [128, TILE])
        acc_sb = sb("acc_sb", [128, TILE])
        rcp = sb("rcp", [128, NB, 4])
        o_y = sb("o_y", [128, NB, D])

        att = ExitStack()
        w_raw = sb("w_raw", [128, 2 * MB * HID], stack=att)
        v_all = sb("v_all", [128, KB, NQ, 4 * VW], stack=att)
        v_quad = sb("v_quad", [128, KB, 4, VW], stack=att)
        k_st = sb("k_st", [ROWS, NT, 4 * TILE], BF16, stack=att)
        q_st = sb("q_st", [ROWS, NT, 4 * TILE], BF16, stack=att)
        msk = sb("msk", [128, 128], stack=att)
        zeros = sb("zeros", [128, NB * 4 * VW], stack=att)
        up_sb = sb("up_sb", [128, 512], F32R, stack=att)
        lo_rows = sb("lo_rows", [128, 1], stack=att)
        proj = ExitStack()
        wd_sb = sb("wd_sb", [128, 3 * 128], stack=proj)
        up_raw = sb("up_raw", [128, 512], stack=proj)
        xn = sb("xn", [128, KB, D], stack=proj)
        xnT = sb("xnT", [128, 2, TILE], stack=proj)
        tab = sb("tab", [128, NT, 2, TILE], stack=proj)
        up_hi = sb("up_hi", [128, 512], F32R, stack=proj)
        c_sb = [sb(f"c{i}_sb", [128, TILE], F32R, stack=proj) for i in range(2)]
        proj.close()
        p_sb = sb("p_sb", [128, PBUF, 4, TILE], stack=att)
        att.close()

        ffn = ExitStack()
        g_h = [sb(f"g{i}h", [128, MB, TILE], F32R, stack=ffn) for i in range(3)]
        g_l = [sb(f"g{i}l", [128, MB, TILE], F32R, stack=ffn) for i in range(3)]
        g_f = [sb(f"gf{i}", [128, TILE], stack=ffn) for i in range(4)]
        t_f = [sb(f"tf{i}", [128, TILE], stack=ffn) for i in range(2)]
        r_f = [sb(f"rf{i}", [128, TILE], stack=ffn) for i in range(2)]
        u_f = [sb(f"uf{i}", [128, TILE], stack=ffn) for i in range(2)]
        ffn.close()

        ps = ctx.enter_context(nc.psum_tensor("ps", [128, 8, TILE], F32))
        B_TR, B_C, B_RA, B_RB, B_QC, B_KC, B_V = 0, 1, 3, 4, 5, 6, 7
        B_ACC = 6
        B_MID = [7, 6, 6, 7]
        B_FLAG, B_XT, B_YT = 6, 6, 7

        qk_dram = [nc.dram_tensor(f"qk_parts{t}", [2, NQ, PARTS, DQK, 4, TILE], BF16).ap() for t in range(NT)]

        x_in = [sem(f"x_in{t}") for t in range(NT)]
        tab_in = [sem(f"tab_in{t}") for t in range(NT)]
        id_in = sem("id_in")
        wd_in = sem("wd_in")
        up_in = sem("up_in")
        late_in = sem("late_in")
        ffnw_in = [sem(f"ffnw_in{i}") for i in range(2)]
        up_split = sem("up_split")
        lo_rows_set = sem("lo_rows_set")
        ffnw_split = sem("ffnw_split")
        filled = sem("filled")
        stats_done = sem("stats_done")
        stats_seen = sem("stats_seen")
        mv_done = sem("mv_done")
        var_ready = sem("var_ready")
        rstd_ready = sem("rstd_ready")
        scales_ready = sem("scales_ready")
        xn_ready = sem("xn_ready")
        tr_done = sem("tr_done")
        xnT_ready = sem("xnT_ready")
        down_done = sem("down_done")
        c_hi = sem("c_hi")
        c_lo = sem("c_lo")
        up_done = sem("up_done")
        v_copied = sem("v_copied")
        rope_mul = sem("rope_mul")
        rope_done = sem("rope_done")
        part0 = [sem(f"part0_{n}") for n in range(3)]
        resid0 = [sem(f"resid0_{n}") for n in range(3)]
        part1 = [sem(f"part1_{n}") for n in range(3)]
        part2 = [sem(f"part2_{n}") for n in range(3)]
        parts_out = [sem(f"parts_out{t}") for t in range(NT)]
        k_in = [sem(f"k_in{t}") for t in range(NT)]
        q_in = [sem(f"q_in{t}") for t in range(NT)]
        v_in = sem("v_in")
        scores_done = sem("scores_done")
        exp_done = sem("exp_done")
        clip_done = sem("clip_done")
        pv_done = sem("pv_done")
        acc_zero = sem("acc_zero")
        acc_out = sem("acc_out")
        accT_done = sem("accT_done")
        rcp_done = sem("rcp_done")
        attn_done = sem("attn_done")
        lo_step = sem("lo_step")
        flag_mm = sem("flag_mm")
        flag_ready = sem("flag_ready")
        at_done = sem("at_done")
        attnT_ready = sem("attnT_ready")
        wo_done = sem("wo_done")
        y_copied = sem("y_copied")
        ln_sub = sem("ln_sub")
        ln_mul = sem("ln_mul")
        x1_ready = sem("x1_ready")
        xn2_sub = sem("xn2_sub")
        xn2_ready = sem("xn2_ready")
        t2_done = sem("t2_done")
        xTh_ready = sem("xTh_ready")
        xTl_ready = sem("xTl_ready")
        ff_mm = sem("ff_mm")
        ff_act = sem("ff_act")
        ff_dve = sem("ff_dve")
        g_low = sem("g_low")
        u_low = sem("u_low")
        uh_ready = sem("uh_ready")
        yT_done = sem("yT_done")
        o_ready = sem("o_ready")
        oy_copied = sem("oy_copied")
        o_out = sem("o_out")

        block = ctx.enter_context(nc.Block())

        DOWNS, UPS = 4, 5
        OUTS = 3 * PARTS
        FILLS = 6

        def run(extra, key):
            for what, *args in extra.get(key, []):
                what(*args)

        def run_between(extra, t, stage, m):
            if isinstance(t, int):
                run(extra, (t, stage, m))

        def ffn_tiles(eng, segment):
            segment(-1, "first", None)
            segment(0, "mid", "first")
            with eng.Fori(1, NT - 1) as t:
                segment(t, "mid", "mid")
            segment(NT - 1, "last", "mid")

        def products(kind):
            return [(pos, stage, m) for pos, (stage, m, _) in enumerate(FFN_PLAN) if (kind, "mm", pos) in AT]

        def base(name, t):
            return 0 if isinstance(t, int) and t < 0 else t * TOTAL["mid", name] + TOTAL["first", name]

        def done(name, t, kind, prev, pos, before=False):
            if not before:
                return base(name, t) + AT[kind, name, pos] if (kind, name, pos) in AT else None
            if prev is None or (prev, name, pos) not in AT:
                return None
            return base(name, t) - (TOTAL[prev, name] - AT[prev, name, pos])

        def gelu_buffer(pos):
            return [p for p, (stage, _, _) in enumerate(FFN_PLAN) if stage in ("h1", "h2")].index(pos) % len(g_f)

        def earlier(stages, pos, step, n_all):
            order = [p for p, (stage, _, _) in enumerate(FFN_PLAN) if stage in stages]
            i = order.index(pos) - step
            return order[i % n_all], i < 0

        def wait(eng, semaphore, value):
            if not isinstance(value, int) or value > 0:
                eng.wait_ge(semaphore, value)

        def quads(eng, step, tail):
            for s in range(EDGE):
                step(0, s)
            with eng.Fori(0, NQ - 1) as q:
                for s in range(EDGE, NSTEP):
                    step(q, s)
                for s in range(EDGE):
                    step(q + 1, s)
            for s in range(EDGE, NSTEP):
                step(NQ - 1, s)
            tail()

        @block.sync
        def _(sp):
            x_t = x.rearrange("o (t n p) d -> t p (o n) d", t=NT, p=128)

            def load_x(t):
                sp.dma_start(x_sb[:, NB * t:NB * (t + 1), :], x_t[t]).then_inc(x_in[t], 16)

            def load_table(t):
                sp.dma_start(tab[:, t, :, :], table[:, :, t * TILE:(t + 1) * TILE].rearrange("g p n -> p g n")).then_inc(tab_in[t], 16)

            load_x(0)
            sp.dma_start(id_sb[:], ident).then_inc(id_in, 16)
            sp.dma_start(wd_sb[:], wdown).then_inc(wd_in, 16)
            sp.dma_start(up_raw[:], wup).then_inc(up_in, 16)
            load_x(1)
            load_table(0)
            load_x(2)
            load_x(3)
            for t in range(1, NT):
                load_table(t)
            sp.dma_start(msk[:], mask).then_inc(late_in, 16)
            sp.dma_start(wo_sb[:], wo).then_inc(late_in, 16)
            sp.dma_start(sc_sb[:], scales).then_inc(late_in, 16)

            def load_q(quad, t):
                src = qk_dram[t][0, bass.ds(quad, 1)].rearrange("o i d h n -> (o i d) (h n)")
                sp.dma_start(q_st[:, t, :], src.unsqueeze(1).to_broadcast([PARTS * DQK, PARTS, 4 * TILE])).then_inc(q_in[t], 16)

            def load_k(quad, t):
                for i in range(PARTS):
                    src = qk_dram[t][1, bass.ds(quad, 1)].rearrange("o j d h n -> (o d) j (h n)")
                    sp.dma_start(k_st[i * PARTS * DQK:(i + 1) * PARTS * DQK, t, :], src).then_inc(k_in[t], 16)

            def load_first(t):
                sp.wait_ge(parts_out[t], 16 * OUTS)
                load_k(0, t)
                load_q(0, t)

            def store_part(t, n, i):
                sp.wait_ge((part0, part1, part2)[i][n], t + 1)
                if n < 2:
                    dst = qk_dram[t][n, :, i, 0:DH]
                else:
                    dst = qk_dram[t][:, :, i, DH:DQK].rearrange("x q d h n -> (x q) d h n")
                sp.dma_start(dst.rearrange("q d h n -> q (d h) n"), parts[n][t % 2][:, i, :]).then_inc(parts_out[t], 16)

            for t in range(NT):
                for nth, (n, i) in enumerate(((0, 0), (1, 0), (0, 1), (1, 1), (2, 0), (0, 2), (1, 2), (2, 1), (2, 2))):
                    store_part(t, n, i)
                    if nth == 3 and t > 0:
                        load_first(t - 1)
            load_first(NT - 1)
            sp.dma_start(w_raw[:, 0:2 * HID].rearrange("p (g m) -> p g m", g=2), w12.rearrange("g p m -> p g m")).then_inc(ffnw_in[0], 16)
            sp.dma_start(w_raw[:, 2 * HID:2 * HID + MB * D].rearrange("p (k m) -> p k m", k=MB),
                         w3.rearrange("(k p) m -> p k m", p=128)).then_inc(ffnw_in[0], 16)
            sp.wait_ge(ffnw_split, 4)
            sp.dma_start(w_raw[:, :].rearrange("p (g k m) -> p g k m", g=2, k=MB),
                         h12.rearrange("g (k p) m -> p g k m", p=128)).then_inc(ffnw_in[1], 16)
            with sp.Fori(0, NQ - 1) as q:
                for t in range(NT - 1):
                    sp.wait_ge(scores_done, q * (2 * NSTEP) + 2 * LAST[t])
                    load_q(q + 1, t)
                for c in range(NT):
                    sp.wait_ge(scores_done, q * (2 * NSTEP) + 2 * KEYS_USED[c])
                    load_k(q + 1, c)
                load_q(q + 1, NT - 1)

            out_t = out.rearrange("o (n p) d -> p (o n) d", p=128)

            def store(t):
                sp.dma_start(out_t[:, bass.ds(t * NB, NB), :], x1[:, bass.ds(t * NB, NB), :]).then_inc(o_out, 16)

            with sp.Fori(0, NT - 1) as t:
                sp.wait_ge(o_ready, t + 2)
                store(t)
            sp.wait_ge(o_ready, NT + 1)
            store(NT - 1)
            sp.wait_ge(o_out, 16 * NT)

        @block.gpsimd
        def _(pool):
            pool.memset(neg_half[:], -0.5).then_inc(filled, 1)
            pool.memset(v_all[:], 1.0).then_inc(filled, 1)
            pool.memset(zeros[:], 0.0).then_inc(filled, 1)
            pool.memset(ones_col[:], 1.0).then_inc(filled, 1)
            pool.memset(w_lo[:, 11 * HID:].bitcast(F32), 0.0).then_inc(filled, 1)
            pool.wait_ge(filled, 5)

            def inverse_root(nth, slot):
                pool.wait_ge(var_ready, nth + 1)
                pool.tensor_tensor(rstd[:, slot, :], var_eps[:, slot, :], neg_half[:], ALU.pow).then_inc(rstd_ready, 1)

            def last_part(n, t):
                pool.wait_ge(part1[n], t + 1)
                pool.tensor_tensor(parts[n][t % 2][:, 2, :], resid[n][t % 2][:], parts[n][t % 2][:, 1, :],
                                   ALU.subtract).then_inc(part2[n], 1)

            def v_stage(quad, c):
                return pool.tensor_tensor(v_quad[:, NB * c:NB * (c + 1), :, :].rearrange("p k h v -> p k (h v)"),
                                          v_all[:, NB * c:NB * (c + 1), bass.ds(quad, 1), :].rearrange("p k o v -> p k (o v)"),
                                          zeros[:].rearrange("p (k v) -> p k v", k=NB), ALU.add)

            def first_quad_values(c):
                pool.wait_ge(v_copied, c + 1)
                v_stage(0, c).then_inc(v_in, 1)

            inverse_root(0, 0)
            inverse_root(1, 1)
            pool.wait_ge(up_split, 1)
            pool.tensor_tensor(up_sb[:], up_raw[:], up_hi[:].bitcast(F32), ALU.subtract).then_inc(up_split, 1)
            inverse_root(2, 2)
            inverse_root(3, 3)
            for t in range(NT):
                pool.wait_ge(rope_mul, t + 1)
                wait(pool, resid0[2], t)
                pool.tensor_tensor(rope[2][:], rope[0][:], rope[1][:], ALU.add).then_inc(rope_done, 1)
                for n in range(3):
                    if n == 2:
                        first_quad_values(t)
                    last_part(n, t)

            raw12 = w_raw[:, 0:2 * HID].rearrange("p (g m) -> p g m", g=2)
            raw3 = w_raw[:, 2 * HID:2 * HID + MB * D].rearrange("p (k m) -> p k m", k=MB)
            rawh = w_raw[:, :].rearrange("p (g k m) -> p g k m", g=2, k=MB)

            def hi(dst, src):
                zero = zeros[:, 0:1]
                for _ in range(len(src.shape) - 2):
                    zero = zero.unsqueeze(1)
                pool.tensor_tensor(dst, src, zero.to_broadcast(src.shape), ALU.add).then_inc(ffnw_split, 1)

            pool.wait_ge(ffnw_in[0], 32)

            hi(w12h[:], raw12)
            hi(w3h[:], raw3)
            pool.wait_ge(ffnw_split, 2)
            pool.tensor_tensor(w12l, raw12, w12h[:].bitcast(F32), ALU.subtract).then_inc(ffnw_split, 1)
            pool.tensor_tensor(w3l, raw3, w3h[:].bitcast(F32), ALU.subtract).then_inc(ffnw_split, 1)
            pool.wait_ge(ffnw_in[1], 16)
            hi(h12h[:], rawh)
            pool.wait_ge(ffnw_split, 5)
            pool.tensor_tensor(h12l, rawh, h12h[:].bitcast(F32), ALU.subtract).then_inc(ffnw_split, 1)

            with pool.Fori(0, NQ - 1) as q:
                for c in range(NT):
                    pool.wait_ge(pv_done, q * NSTEP + KEYS_USED[c])
                    v_stage(q + 1, c).then_inc(v_in, 1)

            def normalised_add(dst, res, src, y, slot, nth, ready):
                pool.tensor_tensor(y, src, mv[:, slot, :, 0:1].to_broadcast([128, NB, D]), ALU.subtract).then_inc(ln_sub, 1)
                pool.wait_ge(ln_sub, nth + 1)
                pool.tensor_tensor(y, y, rstd[:, slot, :].unsqueeze(2).to_broadcast([128, NB, D]), ALU.mult).then_inc(ln_mul, 1)
                pool.wait_ge(ln_mul, nth + 1)
                pool.tensor_tensor(dst, res, y, ALU.add).then_inc(ready, 1)

            def root(what):
                inverse_root(LN2_NTH[what], LN2_SLOT[what])

            def make_x1(t):
                y, blocks = yb[:, t % 2, :, :], slice(NB * t, NB * (t + 1))
                pool.wait_ge(rstd_ready, LN2_NTH["att", t] + 1)
                normalised_add(x1[:, blocks, :], x_sb[:, blocks, :], y, y, LN2_SLOT["att", t], t, x1_ready)

            def make_xn2(t):
                what = ("ffn", t)
                root(what)
                slot, y, src = LN2_SLOT[what], xn2[:, t % 2, :, :], x1[:, NB * t:NB * (t + 1), :]
                pool.wait_ge(rstd_ready, LN2_NTH[what] + 1)
                wait(pool, t2_done, t - 1)
                pool.tensor_tensor(y, src, mv[:, slot, :, 0:1].to_broadcast([128, NB, D]), ALU.subtract).then_inc(xn2_sub, 1)
                pool.wait_ge(xn2_sub, t + 1)
                pool.tensor_tensor(y, y, rstd[:, slot, :].unsqueeze(2).to_broadcast([128, NB, D]), ALU.mult).then_inc(xn2_ready, 1)

            root(("att", 0))
            make_x1(0)
            make_xn2(0)
            root(("att", 1))
            make_x1(1)
            root(("att", 2))
            make_x1(2)

            pool.sem_inc(o_ready, 1)
            between = {(-1, 3): [(make_xn2, 1), (root, ("att", 3)), (make_x1, 3), (root, ("ffn", 2)), (root, ("ffn", 3))]}

            def gpsimd_segment(t, kind, prev):
                if prev == "mid":
                    inverse_root(t + (3 * NT - 1), 0)
                    pool.wait_ge(rstd_ready, t + 3 * NT)
                    pool.wait_ge(oy_copied, t)
                    o = x1[:, bass.ds((t - 1) * NB, NB), :]
                    normalised_add(o, o, o_y[:], o_y[:], 0, t + (NT - 1), o_ready)
                for pos, stage, m in products(kind):
                    if stage == "up":
                        pool.wait_ge(uh_ready, done("u", t, kind, prev, pos))
                        pool.tensor_tensor(g_l[0][:, m, :], u_f[m % 2][:], g_h[0][:, m, :].bitcast(F32), ALU.subtract).then_inc(u_low, 1)
                        if isinstance(t, int):
                            run(between, (t, m))

            ffn_tiles(pool, gpsimd_segment)
            inverse_root(4 * NT - 1, 0)

        @block.scalar
        def _(act):
            def rope_part(n, t):
                if n == 0:
                    act.wait_ge(rope_done, t + 1)
                    act.activation(parts[2][t % 2][:, 0, :], rope[2][:], ACT.Copy).then_inc(part0[2], 1)
                else:
                    second_part(2, t)

            def second_part(n, t):
                act.wait_ge(resid0[n], t + 1)
                act.activation(parts[n][t % 2][:, 1, :], resid[n][t % 2][:], ACT.Copy).then_inc(part1[n], 1)

            def copy_xnT(t):
                act.wait_ge(tr_done, t + 1)
                wait(act, down_done, DOWNS * (t - 1))
                act.activation(xnT[:, t % 2, :], ps[:, B_TR, :], ACT.Copy).then_inc(xnT_ready, 1)

            act.wait_ge(up_in, 16)
            act.wait_ge(lo_rows_set, 2)
            act.activation(up_hi[:], up_raw[:], ACT.Copy, scale=lo_rows[:]).then_inc(up_split, 1)
            def latent_hi(t, i):
                act.wait_ge(down_done, DOWNS * t + i + 1)
                wait(act, up_done, UPS * t)
                act.activation(c_sb[i][:], ps[:, B_C + i, :], ACT.Copy).then_inc(c_hi, 1)

            copy_xnT(0)
            latent_hi(0, 0)
            latent_hi(0, 1)
            copy_xnT(1)
            for t in range(NT):
                if t > 1:
                    act.wait_ge(parts_out[t - 2], 16 * OUTS)
                for n in range(2):
                    act.wait_ge(up_done, UPS * t + (1, 4)[n])
                    act.activation(parts[n][t % 2][:, 0, :], ps[:, (B_QC, B_KC)[n], :], ACT.Copy).then_inc(part0[n], 1)
                act.wait_ge(up_done, UPS * t + 5)
                act.wait_ge(filled, 2)
                act.activation(v_all[:, NB * t:NB * (t + 1), :, :].rearrange("p n q (h v) -> p n (q h) v", v=VW)[:, :, :, 0:DH],
                               ps[:, B_V, :].rearrange("p (n h v) -> p n h v", n=NB, v=DH), ACT.Copy).then_inc(v_copied, 1)
                for n in range(2):
                    if t + 1 < NT:
                        latent_hi(t + 1, n)
                    second_part(n, t)
                if t + 1 < NT:
                    rope_part(0, t)
                if t + 2 < NT:
                    copy_xnT(t + 2)
                if t + 1 < NT:
                    rope_part(1, t)

            act.wait_ge(rope_mul, NT)
            act.wait_ge(up_done, UPS * NT)

            def exps(q, s):
                t, nth, kb, c0 = STEPS[s]
                wait(act, pv_done, q * NSTEP + (s - PBUF + 1))
                for half in range(2):
                    h = 2 * s + half
                    act.wait_ge(scores_done, q * (2 * NSTEP) + (h + 1))
                    slot = 2 * SLOT[h]
                    act.activation(p_sb[:, s % PBUF, 2 * half:2 * half + 2, c0:], ps[:, slot:slot + 2, c0:],
                                   ACT.Exp, scale=SCALE).then_inc(exp_done, 1)
                if isinstance(q, int) and (q, s) in ((0, 1), (0, 3)):
                    rope_part(s // 2, NT - 1)

            quads(act, exps, lambda: None)

            def evacuate_last():
                act.wait_ge(pv_done, NQ * NSTEP)
                act.wait_ge(accT_done, NQ * NT - 1)
                act.activation(acc_sb[:], ps[:, B_ACC + (NT - 1) % 2, :], ACT.Copy).then_inc(acc_out, 1)

            def ffn_input_hi(t):
                act.wait_ge(t2_done, t + 1)
                act.activation(xTh[:, t * TILE:(t + 1) * TILE], ps[:, B_XT, :], ACT.Copy).then_inc(xTh_ready, 1)

            def copy_attnT(t):
                act.wait_ge(at_done, t + 1)
                act.wait_ge(wo_done, t)
                act.activation(attnT[:], ps[:, B_MID[t], :], ACT.Copy).then_inc(attnT_ready, 1)

            def gated_hi(m):
                act.wait_ge(ff_dve, done("dve", -1, "first", None, FFN_PLAN.index(("up", m, 1))))
                act.activation(g_h[0][:, m, :], u_f[m % 2][:], ACT.Copy).then_inc(uh_ready, 1)

            between = {
                (-1, "gate", 1): [(gated_hi, 0)], (-1, "gate", 2): [(evacuate_last,), (gated_hi, 1)],
                (-1, "gate", 3): [(gated_hi, 2), (copy_attnT, NT - 1), (gated_hi, 3)], (0, "h1", 1): [(ffn_input_hi, 1)]}
            act.wait_ge(scales_ready, 1)

            def scalar_segment(t, kind, prev):
                for pos, stage, m in products(kind):
                    if stage == "up":
                        continue
                    act.wait_ge(ff_mm, done("mm", t, kind, prev, pos))
                    bank = ps[:, pos % FF_BANKS, :]
                    if stage == "gate":
                        other, before = earlier(("gate",), pos, 2, MB)
                        used = done("dve", t, kind, prev, other, before)
                        if used is not None:
                            act.wait_ge(ff_dve, used)
                        act.activation(t_f[m % 2][:], bank, ACT.Tanh, scale=half_sc[:, 0, m:m + 1]).then_inc(ff_act, 1)
                    elif stage == "down":
                        if not isinstance(t, int) or t > 0:
                            act.wait_ge(yT_done, t)
                        act.activation(y_sb[:], bank, ACT.Copy, scale=sc_sb[:, 4 * MB:4 * MB + 1]).then_inc(ff_act, 1)
                    else:
                        k, gen = {"h1": (2, 1), "h2": (3, 2)}[stage]
                        other, before = earlier(("h1", "h2"), pos, len(g_f), 2 * MB)
                        used = done("low", t, kind, prev, other, before)
                        if used is not None:
                            act.wait_ge(g_low, used)
                        scale = sc_sb[:, k * MB + m:k * MB + m + 1]
                        act.activation(g_f[gelu_buffer(pos)][:], bank, ACT.Gelu, scale=scale)
                        act.activation(g_h[gen][:, m, :], bank, ACT.Gelu, scale=scale).then_inc(ff_act, 1)
                    run_between(between, t, stage, m)

            ffn_tiles(act, scalar_segment)

        @block.vector
        def _(dve):
            def stats(src, nth, slot):
                for n in range(NB):
                    i = dve.bn_stats(stat[:, slot, n, :], src(n))
                i.then_inc(stats_done, 1)
                dve.wait_ge(stats_done, nth + 1)
                if not isinstance(nth, int):
                    dve.sem_inc(stats_seen, 1)
                for n in range(NB):
                    i = dve.bn_aggr(mv[:, slot, n, :], stat[:, slot, n, :])
                i.then_inc(mv_done, 1)
                dve.wait_ge(mv_done, nth + 1)
                dve.tensor_scalar(var_eps[:, slot, :], mv[:, slot, :, 1], EPS, None, ALU.add).then_inc(var_ready, 1)

            def apply_x(dst, src, nth, slot):
                dve.wait_ge(rstd_ready, nth + 1)
                for n in range(NB):
                    i = dve.tensor_scalar(dst(n), src(n), mv[:, slot, n, 0:1], rstd[:, slot, n:n + 1], ALU.subtract, ALU.mult)
                return i

            def stats_x(t):
                dve.wait_ge(x_in[t], 16)
                stats(lambda n: x_sb[:, NB * t + n, :], t, t)

            def norm_x(t):
                apply_x(lambda n: xn[:, NB * t + n, :], lambda n: x_sb[:, NB * t + n, :], t, t).then_inc(xn_ready, 1)

            def residual(n, t):
                dve.wait_ge(part0[n], t + 1)
                wait(dve, part2[n], t - 1)
                src = ps[:, (B_QC, B_KC)[n], :] if n < 2 else rope[2][:]
                dve.tensor_tensor(resid[n][t % 2][:], src, parts[n][t % 2][:, 0, :], ALU.subtract).then_inc(resid0[n], 1)

            dve.memset(lo_rows[:], 0.0).then_inc(lo_rows_set, 1)
            dve.wait_ge(lo_rows_set, 1)
            for g in (1, 3):
                i = dve.memset(lo_rows[32 * g:32 * g + 32, :], 1.0)
            i.then_inc(lo_rows_set, 1)
            stats_x(0)
            stats_x(1)
            norm_x(0)
            norm_x(1)
            stats_x(2)
            stats_x(3)
            for t in range(NT):
                for i in range(2):
                    dve.wait_ge(c_hi, t * 2 + i + 1)
                    dve.tensor_tensor(c_sb[i][64:128, :], ps[64:128, B_C + i, :], c_sb[i][64:128, :].bitcast(F32),
                                      ALU.subtract).then_inc(c_lo, 1)
                if t > 0:
                    residual(2, t - 1)
                dve.wait_ge(tab_in[t], 16)
                dve.wait_ge(down_done, DOWNS * t + 4)
                dve.wait_ge(up_done, UPS * t + 3)
                wait(dve, rope_done, t)
                dve.tensor_tensor(rope[0][:], ps[:, B_RA, :], tab[:, t, 0, :], ALU.mult)
                dve.tensor_tensor(rope[1][:], ps[:, B_RB, :], tab[:, t, 1, :], ALU.mult).then_inc(rope_mul, 1)
                residual(0, t)
                residual(1, t)
                if t + 2 < NT:
                    norm_x(t + 2)
            dve.wait_ge(resid0[1], NT)
            dve.memset(ps[:, B_ACC, :], 0.0).then_inc(acc_zero, 1)
            dve.wait_ge(late_in, 48)
            dve.tensor_scalar(half_sc[:, 0, :], sc_sb[:, 0:MB], 0.5, None, ALU.mult)
            dve.scalar_tensor_tensor(half_sc[:, 1, :], sc_sb[:, 0:MB], 0.5, sc_sb[:, MB:2 * MB], ALU.mult, ALU.mult).then_inc(scales_ready, 1)

            def clip(q, s, half):
                t, nth, kb, c0 = STEPS[s]
                dve.wait_ge(exp_done, q * (2 * NSTEP) + (2 * s + half + 1))
                p = p_sb[:, s % PBUF, 2 * half:2 * half + 2, :]
                if kb < NB * t:
                    i = dve.tensor_scalar(p, p, LO, HI, ALU.max, ALU.min)
                else:
                    d = p[:, :, c0:c0 + 128]
                    i = dve.scalar_tensor_tensor(d, d, LO, msk[:].unsqueeze(1).to_broadcast([128, 2, 128]), ALU.max, ALU.min)
                    if c0 + 128 < TILE:
                        r = p[:, :, c0 + 128:]
                        i = dve.tensor_scalar(r, r, LO, HI, ALU.max, ALU.min)
                i.then_inc(clip_done, 1)

            def evacuate(q, t):
                dve.wait_ge(pv_done, q * NSTEP + LAST[t])
                wait(dve, accT_done, q * NT + t)
                dve.tensor_copy(acc_sb[:], ps[:, B_ACC + t % 2, :]).then_inc(acc_out, 1)

            def normalise(q, t):
                dve.wait_ge(accT_done, q * NT + (t + 1))
                bank = ps[:, B_ACC + t % 2, :].rearrange("p (n h v) -> p n h v", n=NB, h=4)
                dve.reciprocal(rcp[:], bank[:, :, :, DH]).then_inc(rcp_done, 1)
                dve.wait_ge(rcp_done, q * NT + (t + 1))
                dst = attn[:, NB * t:NB * (t + 1), bass.ds(q * (4 * DH), 4 * DH)].rearrange("p n (h v) -> p n h v", h=4)
                dve.tensor_tensor(dst, bank[:, :, :, 0:DH], rcp[:].unsqueeze(3).to_broadcast([128, NB, 4, DH]), ALU.mult).then_inc(attn_done, 1)

            def largest_lo(q, i):
                dve.wait_ge(ffnw_split, 6)
                n = q * len(LO_STEPS) + i
                dve.tensor_reduce(lo_max[:, bass.ds(n, 1)], w_lo[:, bass.ds(n * LO_COLS, LO_COLS)].bitcast(F32), mybir.AxisListType.X,
                                  ALU.max, apply_absolute_value=True).then_inc(lo_step, 1)

            def all_lo():
                dve.wait_ge(lo_step, LO_PIECES)
                dve.tensor_reduce(lo_any[:], lo_max[:], mybir.AxisListType.X, ALU.max).then_inc(lo_step, 1)

            def any_lo():
                dve.wait_ge(lo_step, LO_PIECES + 1)
                dve.tensor_scalar(lo_any[:], lo_any[:], 0.0, None, ALU.is_gt).then_inc(lo_step, 1)

            def copy_attnT(t):
                dve.wait_ge(at_done, t + 1)
                wait(dve, wo_done, t)
                dve.tensor_copy(attnT[:], ps[:, B_MID[t], :]).then_inc(attnT_ready, 1)

            def take_y(t):
                dve.wait_ge(wo_done, t + 1)
                wait(dve, x1_ready, t - 1)
                dve.tensor_copy(yb[:, t % 2, :, :].rearrange("p n d -> p (n d)"), ps[:, B_MID[t], :]).then_inc(y_copied, 1)

            def stats_att(t):
                dve.wait_ge(y_copied, t + 1)
                stats(lambda n: yb[:, t % 2, n, :], LN2_NTH["att", t], LN2_SLOT["att", t])

            def stats_ffn(t):
                dve.wait_ge(x1_ready, t + 1)
                stats(lambda n: x1[:, t * NB + n, :], LN2_NTH["ffn", t], LN2_SLOT["ffn", t])

            def norm_ffn(t):
                wait(dve, t2_done, t - 1)
                apply_x(lambda n: xn2[:, t % 2, n, :], lambda n: x1[:, t * NB + n, :], LN2_NTH["ffn", t], LN2_SLOT["ffn", t]).then_inc(xn2_ready, 1)

            def ffn_input(t):
                cols = slice(t * TILE, (t + 1) * TILE)
                dve.wait_ge(t2_done, t + 1)
                if t != 1:
                    dve.tensor_copy(xTh[:, cols], ps[:, B_XT, :]).then_inc(xTh_ready, 1)
                dve.wait_ge(xTh_ready, t + 1)
                dve.tensor_tensor(xTl[:, cols], ps[:, B_XT, :], xTh[:, cols].bitcast(F32), ALU.subtract).then_inc(xTl_ready, 1)

            def copy_flag():
                dve.wait_ge(flag_mm, 1)
                dve.tensor_copy(lo_flag[:], ps[0:1, B_FLAG, 0:1]).then_inc(flag_ready, 1)

            vector_extra = {
                (1, 3): [(all_lo,)], (1, 4): [(any_lo,)], (1, 6): [(copy_flag,)], (2, 4): [(copy_attnT, 0)], (2, 6): [(take_y, 0)],
(3, 0): [(stats_att, 0)], (3, 4): [(copy_attnT, 1)], (3, 5): [(stats_ffn, 0)],(3, 6): [(take_y, 1)], (3, 7): [(stats_att, 1)], (3, 9): [(ffn_input, 0)], (3, 11): [(copy_attnT, 2)],(3, 13): [(take_y, 2)], (3, 14): [(stats_att, 2)]}

            def vector_step(q, s):
                t, nth, kb, c0 = STEPS[s]
                for half in range(2):
                    clip(q, s, half)
                if isinstance(q, int) and q == NQ - 1:
                    run(vector_extra, (t, nth))
                elif s in LO_STEPS:
                    largest_lo(q, LO_STEPS.index(s))
                prev = isinstance(q, int) and q == 0
                if prev and s == 1:
                    dve.wait_ge(v_copied, NT)
                    dve.memset(ps[:, B_ACC + 1, :], 0.0).then_inc(acc_zero, 1)
                if prev and s == 2:
                    residual(2, NT - 1)
                if s == EVACUATE and not prev:
                    evacuate(q - 1, NT - 1)
                if s == NORMALISE and not prev:
                    normalise(q - 1, NT - 1)
                if t > 0 and nth == EVACUATE:
                    evacuate(q, t - 1)
                if t > 0 and nth == NORMALISE:
                    normalise(q, t - 1)

            quads(dve, vector_step, lambda: None)

            between = {
                (-1, "up", 2): [(normalise, NQ - 1, NT - 1)], (-1, "up", 3): [(stats_ffn, 1)], (-1, "h1", 0): [(take_y, 3), (stats_att, 3)],
                (0, "h1", 1): [(ffn_input, 1)], (0, "h1", 2): [(stats_ffn, 2)], (0, "h1", 3): [(stats_ffn, 3)], (0, "up", 1): [(norm_ffn, 2)],
                (0, "h2", 2): [(ffn_input, 2)], (0, "h2", 3): [(norm_ffn, 3)], (0, "down", 0): [(ffn_input, 3)]}

            def output_stats(t):
                dve.wait_ge(yT_done, t + 1)
                dve.wait_ge(o_ready, t + 1)
                if not isinstance(t, int) or t < NT - 1:
                    dve.tensor_copy(o_y[:].rearrange("p n d -> p (n d)"), ps[:, B_YT, :]).then_inc(oy_copied, 1)
                stats(lambda n: ps[:, B_YT, n * D:(n + 1) * D], t + 3 * NT, 0)

            def vector_segment(t, kind, prev):
                for pos, stage, m in products(kind):
                    bank = ps[:, pos % FF_BANKS, :]
                    if stage == "gate":
                        dve.wait_ge(ff_act, done("act", t, kind, prev, pos))
                        dve.scalar_tensor_tensor(r_f[m % 2][:], t_f[m % 2][:], 1.0, bank, ALU.add, ALU.mult).then_inc(ff_dve, 1)
                    elif stage == "up":
                        dve.wait_ge(ff_mm, done("mm", t, kind, prev, pos))
                        dve.wait_ge(ff_dve, done("dve", t, kind, prev, pos - 1))
                        other, before = earlier(("up",), pos, 2, MB)
                        used = done("u", t, kind, prev, other, before)
                        if used is not None:
                            dve.wait_ge(u_low, used)
                        dve.scalar_tensor_tensor(u_f[m % 2][:], bank, half_sc[:, 1, m:m + 1], r_f[m % 2][:], ALU.mult, ALU.mult).then_inc(ff_dve, 1)
                        if kind == "first":
                            run_between(between, t, stage, m)
                            continue
                        dve.wait_ge(ff_dve, done("dve", t, kind, prev, pos))
                        dve.tensor_copy(g_h[0][:, m, :], u_f[m % 2][:]).then_inc(uh_ready, 1)
                    elif stage in ("h1", "h2"):
                        gen = {"h1": 1, "h2": 2}[stage]
                        dve.wait_ge(ff_act, done("act", t, kind, prev, pos))
                        dve.tensor_tensor(g_l[gen][:, m, :], g_f[gelu_buffer(pos)][:], g_h[gen][:, m, :].bitcast(F32),
                                          ALU.subtract).then_inc(g_low, 1)
                    run_between(between, t, stage, m)
                    if pos == 0 and prev == "mid":
                        output_stats(t - 1)

            ffn_tiles(dve, vector_segment)
            output_stats(NT - 1)
            last = slice(NB * (NT - 1), NB * NT)
            apply_x(lambda n: o_y[:, n, :], lambda n: ps[:, B_YT, n * D:(n + 1) * D], 4 * NT - 1, 0).then_inc(ln_mul, 1)
            dve.wait_ge(ln_mul, 2 * NT)
            dve.tensor_tensor(x1[:, last, :], x1[:, last, :], o_y[:], ALU.add).then_inc(o_ready, 1)

        @block.tensor
        def _(pe):
            def transpose4(bank, src):
                for n in range(NB):
                    i = pe.transpose(ps[:, bank, n * 128:(n + 1) * 128], src(n), id_sb[:])
                return i

            def turn_x(t):
                pe.wait_ge(xn_ready, t + 1)
                wait(pe, xnT_ready, t)
                transpose4(B_TR, lambda n: xn[:, NB * t + n, :]).then_inc(tr_done, 1)

            pe.wait_ge(id_in, 16)
            turn_x(0)
            pe.wait_ge(wd_in, 16)
            for t in range(NT):
                pe.wait_ge(xnT_ready, t + 1)
                wait(pe, c_lo, t * 2)
                for i in range(2):
                    pe.matmul(ps[:, B_C + i, :], wd_sb[:, i * 128:(i + 1) * 128], xnT[:, t % 2, :], start=True, stop=True).then_inc(down_done, 1)
                wait(pe, rope_mul, t)
                for i in range(2):
                    pe.matmul(ps[64:128, B_RA + i, :], wd_sb[:, 256 + i * 64:256 + (i + 1) * 64], xnT[:, t % 2, :],
                              start=True, stop=True).then_inc(down_done, 1)
                if t + 1 < NT:
                    turn_x(t + 1)
                pe.wait_ge(up_split, 2)
                pe.wait_ge(c_lo, t * 2 + 1)
                wait(pe, resid0[0], t)
                pe.matmul(ps[:, B_QC, :], up_sb[:, 0:128], c_sb[0][:], start=True, stop=True).then_inc(up_done, 1)
                for i in range(2):
                    pe.matmul(ps[0:64, B_RA + i, :], up_sb[:, 128 + i * 64:128 + (i + 1) * 64], c_sb[0][:],
                              start=True, stop=True).then_inc(up_done, 1)
                pe.wait_ge(c_lo, t * 2 + 2)
                wait(pe, resid0[1], t)
                pe.matmul(ps[:, B_KC, :], up_sb[:, 256:384], c_sb[1][:], start=True, stop=True).then_inc(up_done, 1)
                wait(pe, v_copied, t)
                for n in range(NB):
                    i = pe.matmul(ps[:, B_V, n * 128:(n + 1) * 128], c_sb[1][:, n * 128:(n + 1) * 128], up_sb[:, 384:512], start=True, stop=True)
                i.then_inc(up_done, 1)

            def scores(q, h):
                s, half = h // 2, h % 2
                t, nth, kb, c0 = STEPS[s]
                if nth == 0 and half == 0:
                    pe.wait_ge(q_in[t], (q + 1) * 16)
                if kb == NB * t and half == 0:
                    pe.wait_ge(k_in[t], (q + 1) * (16 * PARTS))
                wait(pe, exp_done, q * (2 * NSTEP) + SLOT_USED[h])
                for j in range(2):
                    head = (2 * half + j) * TILE
                    key = head + (kb % NB) * 128
                    i = pe.matmul(ps[:, 2 * SLOT[h] + j, c0:], k_st[:, kb // NB, key:key + 128],
                                  q_st[:, t, head + c0:head + TILE], start=True, stop=True)
                i.then_inc(scores_done, 1)

            def weigh(q, s):
                t, nth, kb, c0 = STEPS[s]
                if isinstance(q, int) and q == 0 and nth == 0 and t < 2:
                    pe.wait_ge(acc_zero, t + 1)
                pe.wait_ge(clip_done, q * (2 * NSTEP) + (2 * s + 2))
                if kb == NB * t:
                    pe.wait_ge(v_in, q * NT + (t + 1))
                if nth == 0:
                    wait(pe, attn_done, q * NT + (t - 1))
                    if isinstance(q, int) and q == NQ - 1 and t > 1:
                        pe.wait_ge(*{2: (flag_ready, 1), 3: (y_copied, 1)}[t])
                for j in range(4):
                    i = pe.matmul(ps[32 * j:32 * j + VW, B_ACC + t % 2, c0:], v_quad[:, kb, j, :], p_sb[:, s % PBUF, j, c0:],
                                  start=(nth == 0), stop=(nth == NB * (t + 1) - 1))
                i.then_inc(pv_done, 1)

            def turn(q, t):
                pe.wait_ge(acc_out, q * NT + (t + 1))
                transpose4(B_ACC + t % 2, lambda n: acc_sb[:, n * 128:(n + 1) * 128]).then_inc(accT_done, 1)

            def turn_attn(t):
                pe.wait_ge(attn_done, (NQ - 1) * NT + (2, 3, 3, 4)[t])
                transpose4(B_MID[t], lambda n: attn[:, t * NB + n, :]).then_inc(at_done, 1)

            def project(t):
                pe.wait_ge(late_in, 48)
                pe.wait_ge(attnT_ready, t + 1)
                for n in range(NB):
                    i = pe.matmul(ps[:, B_MID[t], n * D:(n + 1) * D], attnT[:, n * 128:(n + 1) * 128], wo_sb[:], start=True, stop=True)
                i.then_inc(wo_done, 1)

            def turn_x1(t, bank_free):
                pe.wait_ge(*bank_free)
                pe.wait_ge(xn2_ready, t + 1)
                transpose4(B_XT, lambda n: xn2[:, t % 2, n, :]).then_inc(t2_done, 1)

            def flag_sum():
                pe.wait_ge(lo_step, LO_PIECES + 2)
                pe.wait_ge(attn_done, (NQ - 1) * NT + 1)
                pe.matmul(ps[0:1, B_FLAG, 0:1], lo_any[:], ones_col[:], start=True, stop=True).then_inc(flag_mm, 1)

            def then(semaphore, value, what, *args):
                pe.wait_ge(semaphore, value)
                what(*args)

            tensor_extra = {
                (1, 6): [(flag_sum,)], (2, 4): [(turn_attn, 0)], (2, 6): [(project, 0)],(3, 4): [(turn_attn, 1)], (3, 6): [(project, 1)],
                (3, 9): [(turn_x1, 0, (y_copied, 2))], (3, 11): [(then, xTl_ready, 1, turn_attn, 2)], (3, 13): [(project, 2)]}

            def tensor_step(q, s):
                first = isinstance(q, int) and q == 0
                scores(q, 2 * s)
                scores(q, 2 * s + 1)
                if s >= LAG:
                    weigh(q, s - LAG)
                elif not first:
                    weigh(q - 1, NSTEP + s - LAG)
                t, nth, _, _ = STEPS[s]
                if s == TURN and not first:
                    turn(q - 1, NT - 1)
                if t > 0 and nth == TURN:
                    turn(q, t - 1)
                if isinstance(q, int) and q == NQ - 1:
                    run(tensor_extra, (t, nth))

            pe.wait_ge(xnT_ready, NT)
            pe.wait_ge(c_lo, 2 * NT)
            pe.wait_ge(rope_mul, NT)
            pe.wait_ge(resid0[0], NT)
            quads(pe, tensor_step, lambda: None)

            def product(bank, terms, with_lo):
                n, last = 0, (4 if with_lo else 2) * len(terms) - 1
                for ready, wh, wl, ah, al in terms:
                    if ready is not None:
                        pe.wait_ge(*ready)
                    for w, v in ((wh, ah), (wh, al), (wl, ah), (wl, al))[:4 if with_lo else 2]:
                        i = pe.matmul(ps[:, bank, :], w, v, start=(n == 0), stop=(n == last))
                        n += 1
                i.then_inc(ff_mm, 1)

            between = {
                (-1, "up", 0): [(weigh, NQ - 1, NSTEP - 2)], (-1, "up", 1): [(weigh, NQ - 1, NSTEP - 1)], (-1, "up", 2): [(turn, NQ - 1, NT - 1)], (-1, "up", 3): [(turn_attn, 3)], (-1, "h1", 0): [(project, 3)],
                (0, "h1", 1): [(turn_x1, 1, (y_copied, 3))],
                (0, "h2", 2): [(turn_x1, 2, (xTl_ready, 2))], (0, "down", 0): [(turn_x1, 3, (xTl_ready, 3))]}

            def turn_output(t):
                last = isinstance(t, int) and t == NT - 1
                pe.wait_ge(ff_act, base("act", t) + TOTAL["last" if last else "mid", "act"])
                pe.wait_ge(mv_done, t + 3 * NT)
                transpose4(B_YT, lambda n: y_sb[:, n * 128:(n + 1) * 128]).then_inc(yT_done, 1)

            def tensor_segment(with_lo):
                def segment(t, kind, prev):
                    for pos, stage, m in products(kind):
                        bank = pos % FF_BANKS
                        here = [p for p, _, _ in products(kind) if p < pos and p % FF_BANKS == bank]
                        there = [p for p, _, _ in products(prev) if p % FF_BANKS == bank]
                        if here or there:
                            p = (here or there)[-1]
                            name = "dve" if FFN_PLAN[p][0] in ("gate", "up") else "act"
                            pe.wait_ge({"dve": ff_dve, "act": ff_act}[name], done(name, t, kind, prev, p, not here))
                        else:
                            used = [h for h in range(2 * NSTEP) if SLOT[h] == bank // 2][-1]
                            pe.wait_ge(exp_done, (NQ - 1) * (2 * NSTEP) + (used + 1))
                        cols = slice(m * 128, (m + 1) * 128)
                        low = base("low", t)
                        if stage in ("gate", "up"):
                            g = ("gate", "up").index(stage)
                            tok = bass.ds((t + 1) * TILE, TILE)
                            pe.wait_ge(xTl_ready, t + 2)
                            terms = [(None, w12h[:, g, cols], w12l[:, g, cols], xTh[:, tok], xTl[:, tok])]
                        elif stage == "h1":
                            terms = [((u_low, base("u", t) + (k + 1)) if m == 0 else None, h12h[:, 0, k, cols], h12l[:, 0, k, cols],
                                      g_h[0][:, k, :], g_l[0][:, k, :]) for k in range(MB)]
                        elif stage == "h2":
                            terms = [((g_low, low + k) if m == 0 else None, h12h[:, 1, k, cols], h12l[:, 1, k, cols],
                                      g_h[1][:, k, :], g_l[1][:, k, :]) for k in range(MB)]
                        else:
                            h2 = [p for p, (s, _, _) in enumerate(FFN_PLAN) if s == "h2"]
                            terms = [((g_low, low + AT[kind, "low", h2[k]]), w3h[:, k, :], w3l[:, k, :],
                                      g_h[2][:, k, :], g_l[2][:, k, :]) for k in range(MB)]
                        product(bank, terms, with_lo)
                        run_between(between, t, stage, m)
                        if pos == 0 and prev == "mid":
                            turn_output(t - 1)
                return segment

            pe.wait_ge(flag_ready, 1)
            flag = pe.value_load(lo_flag[0:1, 0:1].bitcast(mybir.dt.int32))
            with pe.If(flag != 0):
                ffn_tiles(pe, tensor_segment(True))
                turn_output(NT - 1)
            with pe.Else():
                ffn_tiles(pe, tensor_segment(False))
                turn_output(NT - 1)


def kernel(L0_attn_x, L0_attn_W_DQ, L0_attn_W_UQ, L0_attn_W_QR, L0_attn_W_DKV, L0_attn_W_UK, L0_attn_W_UV,
           L0_attn_W_KR, L0_attn_W_O, L0_ffn_w1_w, L0_ffn_w1_s, L0_ffn_w2_w, L0_ffn_w2_s, L0_ffn_h1_w, L0_ffn_h1_s,
           L0_ffn_h2_w, L0_ffn_h2_s, L0_ffn_w3_w, L0_ffn_w3_s):
    import concourse.bacc as bacc
    from concourse.bass_utils import run_bass_kernel_spmd

    a = np.asarray
    content = np.arange(H * DH).reshape(NQ, 4, DH).transpose(0, 2, 1).reshape(-1)
    rope = np.arange(H * DR).reshape(NQ, 4, DR).transpose(0, 2, 1).reshape(-1)
    dim = rope % DR
    uq, qr, uk, kr = a(L0_attn_W_UQ), a(L0_attn_W_QR), a(L0_attn_W_UK), a(L0_attn_W_KR)
    wup = np.concatenate([uq[:, content], qr[:, rope], qr[:, rope ^ 1], uk[:, content], a(L0_attn_W_UV)], axis=1)
    inv = np.float32(10000.0) ** (-np.arange(0, DR, 2, dtype=np.float32) / np.float32(DR))
    angle = (np.arange(S, dtype=np.float32)[:, None] * inv).T.astype(np.float64)
    cos = np.repeat(np.cos(angle), 2, axis=0)
    sin = np.repeat(np.sin(angle), 2, axis=0) * np.array([-1.0, 1.0, -1.0, 1.0])[:, None]
    arrays = {
        "x": a(L0_attn_x),
        "wdown": np.concatenate([np.tile(a(L0_attn_W_DQ), (1, 4)), np.tile(a(L0_attn_W_DKV), (1, 4)), kr[:, dim], kr[:, dim ^ 1]], axis=1),
        "wup": np.tile(wup, (4, 1)),
        "table": np.stack([np.tile(cos[dim], (2, 1)), np.tile(sin[dim], (2, 1))]).astype(np.float32),
        "ident": np.eye(128, dtype=np.float32),
        "mask": np.where(np.arange(128)[None, :] >= np.arange(128)[:, None], np.float32(HI), np.float32(0)),
        "wo": a(L0_attn_W_O),
        "w12": np.stack([a(L0_ffn_w1_w).T, a(L0_ffn_w2_w).T]),
        "h12": np.stack([a(L0_ffn_h1_w).T, a(L0_ffn_h2_w).T]),
        "w3": a(L0_ffn_w3_w).T,
        "scales": np.concatenate([a(v).reshape(-1, 128) for v in (L0_ffn_w1_s, L0_ffn_w2_s, L0_ffn_h1_s, L0_ffn_h2_s, L0_ffn_w3_s)]).T,
    }
    nc = bacc.Bacc("TRN2", target_bir_lowering=False, num_devices=1)
    ins, args = {}, {}
    for name, v in arrays.items():
        v = np.ascontiguousarray(v)
        ins["in_" + name] = v
        args[name] = nc.dram_tensor("in_" + name, v.shape, F32, kind="ExternalInput").ap()
    args["out"] = nc.dram_tensor("out", (1, S, D), F32, kind="ExternalOutput").ap()
    build(nc, **args)
    r = run_bass_kernel_spmd(nc, [ins], core_ids=[0])
    return r.results[0]["out"]
```
